# Optimizing a Trainium2 kernel written in Bass

```python
import numpy as np
import jax
import jax.numpy as jnp

def _softmax(x, axis=-1):
    return jax.nn.softmax(x, axis=axis)

def _gelu(x):
    return jax.nn.gelu(x, approximate=True)

def _silu(x):
    return jax.nn.silu(x)

def _sigmoid(x):
    return jax.nn.sigmoid(x)

def _layernorm(x, axis=-1, eps=1e-05):
    m = jnp.mean(x, axis=axis, keepdims=True)
    v = jnp.var(x, axis=axis, keepdims=True)
    return (x - m) / jnp.sqrt(v + eps)

def _scatter_add(tgt, idx, src, axis=0):
    return tgt.at[idx].add(src)

def _segment_sum(src, seg, n):
    return jax.ops.segment_sum(src, seg, n)
kernel_name = 'mk_sandwich_d1_jaxref_r8_6a41fa'

def setup_inputs(seed: int=0):
    np.random.seed(seed)
    _w = jnp.asarray

    def _L0_attn_setup():
        import jax, jax.numpy as jnp
        import numpy as np
        D_MODEL = 128
        NUM_HEADS = 16
        D_K = D_MODEL // NUM_HEADS
        key = jax.random.key(seed)
        ks = jax.random.split(key, 9)
        B, T = (2, 256)
        s = 1.0 / np.sqrt(D_MODEL)
        return {'x': jax.random.normal(ks[0], (B, T, D_MODEL), dtype=jnp.float32), 'w_q': jax.random.normal(ks[1], (D_MODEL, D_MODEL), dtype=jnp.float32) * s, 'b_q': jnp.zeros((D_MODEL,), dtype=jnp.float32), 'w_k': jax.random.normal(ks[2], (D_MODEL, D_MODEL), dtype=jnp.float32) * s, 'b_k': jnp.zeros((D_MODEL,), dtype=jnp.float32), 'w_v': jax.random.normal(ks[3], (D_MODEL, D_MODEL), dtype=jnp.float32) * s, 'b_v': jnp.zeros((D_MODEL,), dtype=jnp.float32), 'w_o': jax.random.normal(ks[4], (D_MODEL, D_MODEL), dtype=jnp.float32) * s, 'b_o': jnp.zeros((D_MODEL,), dtype=jnp.float32)}
    _L0_attn_in = _L0_attn_setup()

    def _L0_ffn_setup():
        import jax, jax.numpy as jnp
        import numpy as np
        HIDDEN = 128
        MOE_INTER = 64
        SHARED_INTER = 256
        N_EXPERTS = 32
        TOP_K = 6
        N_GROUP = 8
        TOPK_GROUP = 4
        ROUTED_SCALE = 2.5

        def _relu2(x):
            return jnp.square(jax.nn.relu(x))

        def _router(x, gate_w, e_bias):
            T = x.shape[0]
            logits = x.astype(jnp.float32) @ gate_w.astype(jnp.float32).T
            scores = jax.nn.sigmoid(logits)
            sc = scores + e_bias[None, :]
            g = sc.reshape(T, N_GROUP, N_EXPERTS // N_GROUP)
            group_scores = jax.lax.top_k(g, 2)[0].sum(-1)
            group_idx = jax.lax.top_k(group_scores, TOPK_GROUP)[1]
            group_mask = jnp.zeros_like(group_scores).at[jnp.arange(T)[:, None], group_idx].set(1.0)
            score_mask = jnp.repeat(group_mask, N_EXPERTS // N_GROUP, axis=1)
            masked = jnp.where(score_mask > 0, sc, 0.0)
            topk_idx = jax.lax.stop_gradient(jax.lax.top_k(masked, TOP_K)[1])
            topk_w = jnp.take_along_axis(scores, topk_idx, axis=1)
            topk_w = topk_w / (topk_w.sum(-1, keepdims=True) + 1e-20)
            topk_w = topk_w * ROUTED_SCALE
            return (topk_idx, topk_w)
        if __name__ == '__main__':
            out = reference(**setup_inputs())
            print(out.shape, out.dtype)
        key = jax.random.key(seed)
        ks = jax.random.split(key, 6)
        s = 0.02
        return {'hidden_states': jax.random.normal(ks[0], (2, 128, HIDDEN), jnp.float32), 'gate_w': jax.random.normal(ks[1], (N_EXPERTS, HIDDEN), jnp.float32) * s, 'e_bias': jnp.zeros((N_EXPERTS,), jnp.float32), 'up_w': jax.random.normal(ks[2], (N_EXPERTS, MOE_INTER, HIDDEN), jnp.float32) * s, 'down_w': jax.random.normal(ks[3], (N_EXPERTS, HIDDEN, MOE_INTER), jnp.float32) * s, 'shared_up_w': jax.random.normal(ks[4], (SHARED_INTER, HIDDEN), jnp.float32) * s, 'shared_down_w': jax.random.normal(ks[5], (HIDDEN, SHARED_INTER), jnp.float32) * s}
    _L0_ffn_in = _L0_ffn_setup()
    _d = {'L0_attn_x': _L0_attn_in['x'], 'L0_attn_w_q': _L0_attn_in['w_q'], 'L0_attn_b_q': _L0_attn_in['b_q'], 'L0_attn_w_k': _L0_attn_in['w_k'], 'L0_attn_b_k': _L0_attn_in['b_k'], 'L0_attn_w_v': _L0_attn_in['w_v'], 'L0_attn_b_v': _L0_attn_in['b_v'], 'L0_attn_w_o': _L0_attn_in['w_o'], 'L0_attn_b_o': _L0_attn_in['b_o'], 'L0_ffn_gate_w': _L0_ffn_in['gate_w'], 'L0_ffn_e_bias': _L0_ffn_in['e_bias'], 'L0_ffn_up_w': _L0_ffn_in['up_w'], 'L0_ffn_down_w': _L0_ffn_in['down_w'], 'L0_ffn_shared_up_w': _L0_ffn_in['shared_up_w'], 'L0_ffn_shared_down_w': _L0_ffn_in['shared_down_w']}
    _x0 = _d['L0_attn_x']
    _d['L0_attn_x'] = jax.random.normal(jax.random.fold_in(jax.random.key(seed), 1), (16, 256, 128), dtype=_x0.dtype)
    del _x0
    return _d

def reference(L0_attn_x, L0_attn_w_q, L0_attn_b_q, L0_attn_w_k, L0_attn_b_k, L0_attn_w_v, L0_attn_b_v, L0_attn_w_o, L0_attn_b_o, L0_ffn_gate_w, L0_ffn_e_bias, L0_ffn_up_w, L0_ffn_down_w, L0_ffn_shared_up_w, L0_ffn_shared_down_w):

    def _L0_attn_ref(x, w_q, b_q, w_k, b_k, w_v, b_v, w_o, b_o):
        import jax, jax.numpy as jnp
        import numpy as np
        D_MODEL = 128
        NUM_HEADS = 16
        D_K = D_MODEL // NUM_HEADS
        B, T, D = x.shape
        H, dk = (NUM_HEADS, D_K)

        def proj(w, b):
            y = jnp.einsum('btd,ed->bte', x, w) + b
            return y.reshape(B, T, H, dk).transpose(0, 2, 1, 3)
        q = proj(w_q, b_q)
        k = proj(w_k, b_k)
        v = proj(w_v, b_v)
        scores = jnp.einsum('bhtd,bhsd->bhts', q, k) / jnp.sqrt(jnp.float32(dk))
        attn = jax.nn.softmax(scores, axis=-1)
        out = jnp.einsum('bhts,bhsd->bhtd', attn, v)
        out = out.transpose(0, 2, 1, 3).reshape(B, T, D)
        return jnp.einsum('btd,ed->bte', out, w_o) + b_o

    def _L0_ffn_ref(hidden_states, gate_w, e_bias, up_w, down_w, shared_up_w, shared_down_w):
        import jax, jax.numpy as jnp
        import numpy as np
        HIDDEN = 128
        MOE_INTER = 64
        SHARED_INTER = 256
        N_EXPERTS = 32
        TOP_K = 6
        N_GROUP = 8
        TOPK_GROUP = 4
        ROUTED_SCALE = 2.5

        def _relu2(x):
            return jnp.square(jax.nn.relu(x))

        def _router(x, gate_w, e_bias):
            T = x.shape[0]
            logits = x.astype(jnp.float32) @ gate_w.astype(jnp.float32).T
            scores = jax.nn.sigmoid(logits)
            sc = scores + e_bias[None, :]
            g = sc.reshape(T, N_GROUP, N_EXPERTS // N_GROUP)
            group_scores = jax.lax.top_k(g, 2)[0].sum(-1)
            group_idx = jax.lax.top_k(group_scores, TOPK_GROUP)[1]
            group_mask = jnp.zeros_like(group_scores).at[jnp.arange(T)[:, None], group_idx].set(1.0)
            score_mask = jnp.repeat(group_mask, N_EXPERTS // N_GROUP, axis=1)
            masked = jnp.where(score_mask > 0, sc, 0.0)
            topk_idx = jax.lax.stop_gradient(jax.lax.top_k(masked, TOP_K)[1])
            topk_w = jnp.take_along_axis(scores, topk_idx, axis=1)
            topk_w = topk_w / (topk_w.sum(-1, keepdims=True) + 1e-20)
            topk_w = topk_w * ROUTED_SCALE
            return (topk_idx, topk_w)
        if __name__ == '__main__':
            out = reference(**setup_inputs())
            print(out.shape, out.dtype)
        B, S, H = hidden_states.shape
        x = hidden_states.reshape(-1, H)
        T = x.shape[0]
        topk_idx, topk_w = _router(x, gate_w, e_bias)
        combine = jnp.zeros((T, N_EXPERTS), topk_w.dtype).at[jnp.arange(T)[:, None], topk_idx].add(topk_w)
        h = _relu2(jnp.einsum('th,eih->tei', x, up_w))
        h = h * combine[:, :, None]
        moe_out = jnp.einsum('tei,ehi->th', h, down_w)
        shared = _relu2(x @ shared_up_w.T) @ shared_down_w.T
        return (moe_out + shared).reshape(B, S, H)
    x = L0_attn_x
    x = x + _layernorm(_L0_attn_ref(_layernorm(x, axis=-1), L0_attn_w_q, L0_attn_b_q, L0_attn_w_k, L0_attn_b_k, L0_attn_w_v, L0_attn_b_v, L0_attn_w_o, L0_attn_b_o), axis=-1)
    x = x + _layernorm(_L0_ffn_ref(_layernorm(x, axis=-1), L0_ffn_gate_w, L0_ffn_e_bias, L0_ffn_up_w, L0_ffn_down_w, L0_ffn_shared_up_w, L0_ffn_shared_down_w), axis=-1)
    return x

_drawn_inputs = setup_inputs


def setup_inputs(seed=0):
    import zlib

    import numpy as np

    out = dict(_drawn_inputs(seed))
    spreads = {'L0_attn_b_q': (0.0, 0.1),
     'L0_attn_b_k': (0.0, 0.1),
     'L0_attn_b_v': (0.0, 0.1),
     'L0_attn_b_o': (0.0, 0.1),
     'L0_ffn_e_bias': (0.0, 0.1)}
    factors = {}
    for name, (base, spread) in spreads.items():
        noise = np.random.default_rng([zlib.crc32(name.encode()), seed]).standard_normal(out[name].shape)
        drawn = base * np.exp(spread * noise) if base else spread * noise
        out[name] = jnp.asarray(drawn.astype(out[name].dtype))
    for name, factor in factors.items():
        out[name] = (out[name] * factor).astype(out[name].dtype)
    return out
```

```python
from contextlib import ExitStack

import numpy as np

import concourse.bass as bass
from concourse import mybir

F32 = mybir.dt.float32
BF16 = mybir.dt.bfloat16
I32 = mybir.dt.int32
ALU = mybir.AluOpType
ACT = mybir.ActivationFunctionType
AX = mybir.AxisListType

P = 128
NB, T, D = 16, 256, 128
H, DK = 16, 8
TH = T // P
NT = NB * TH
NBLK = H // 2
UB = NBLK // 2
NU = 2 * NB
SLOTS = 6
Q_PARTS = (0, 0, 0, 1, 1, 2)
K_PARTS = (0, 1, 2, 0, 1, 0)
QK_ROWS = SLOTS * DK
M_ROWS = 3
HR = 64
RING = 4
SCALE = float(DK) ** -0.5
VC = 32

E, EI, GROUPS, TOPG, TOPK = 32, 64, 8, 4, 6
ROUTED_SCALE = 2.5
SI = 256
TILE = 512
NTILE = NB * T // TILE
C4 = TILE // P
RBLK = E * EI // P
FBLK = RBLK + SI // P
HRING = 3
LAG = 2
EPS = 1e-5
RSQRT_MAGIC = 0x5F3759DF
LN_LINKS = 16
RT_LINKS = 38


class Link:

    def __init__(self, eng, sem, base):
        self.eng, self.sem, self.base, self.n = eng, sem, base, 0

    def __call__(self, instruction):
        self.n += 1
        instruction.then_inc(self.sem, 1)
        self.eng.wait_ge(self.sem, self.base + self.n)


def block_kernel(nc, x, wq, wk, wv, wo, bq, bk, bv, bo, gate, ebias, up, shup, down, shdown,
                 ident_f, ident_b, sel, out):
    with ExitStack() as ctx:
        def sb(name, shape, dt=F32):
            return ctx.enter_context(nc.sbuf_tensor(name, shape, dt))

        def ps(name, shape):
            return ctx.enter_context(nc.psum_tensor(name, shape, F32))

        def sem(name):
            return ctx.enter_context(nc.semaphore(name))

        q_scratch = nc.dram_tensor("q_scratch", (NB, SLOTS, 4, DK, UB, T), BF16).ap()
        k_scratch = nc.dram_tensor("k_scratch", (NB, SLOTS, 4, DK, UB, T), BF16).ap()

        xbig = sb("xbig", [P, NT, D])
        ybig = sb("ybig", [P, NT, D])
        wq_sb, wk_sb = sb("wq_sb", [P, D]), sb("wk_sb", [P, D])
        wv_sb, wo_sb = sb("wv_sb", [P, D]), sb("wo_sb", [P, D])
        bqk_sb = sb("bqk_sb", [P, 2])
        bv_sb, bo_sb = sb("bv_sb", [P, TH, D]), sb("bo_sb", [P, TH, D])
        gate_sb = sb("gate_sb", [P, E])
        ebias_sb = sb("ebias_sb", [P, C4, E])
        up_sb = sb("up_sb", [P, FBLK, P])
        down_sb = sb("down_sb", [P, FBLK, D])
        idf, idb = sb("idf", [P, P]), sb("idb", [P, P], BF16)
        sel_sb = sb("sel_sb", [3 * E, RBLK, P], BF16)
        stats = sb("stats", [P, NT, 6])
        rs1, nm1 = sb("rs1", [P, NT]), sb("nm1", [P, NT])
        rs2, nm2 = sb("rs2", [P, C4]), sb("nm2", [P, C4])
        rs3, nm3 = sb("rs3", [P, C4]), sb("nm3", [P, C4])
        rs4, nm4 = sb("rs4", [P, C4]), sb("nm4", [P, C4])
        nw_v, nw_t, nw_m, nw_d = (sb(f"nw_{n}", [P, NT]) for n in "vtmd")
        nw_i = sb("nw_i", [P, NT], I32)
        xn = sb("xn", [P, TH, D])
        xnT = [sb(f"xnT{i}", [P, T]) for i in range(2)]
        q_parts, k_parts = sb("q_parts", [P, 3, T], BF16), sb("k_parts", [P, 3, T], BF16)
        q_rest, k_rest = sb("q_rest", [P, T]), sb("k_rest", [P, T])
        qp = [sb(f"qp{i}", [P, UB, T], BF16) for i in range(RING)]
        kp = [sb(f"kp{i}", [P, UB, T], BF16) for i in range(RING)]
        vv = [sb(f"vv{i}", [P, TH, H, VC]) for i in range(2)]
        mneg = [sb(f"mneg{i}", [P, TH, 2, UB]) for i in range(2)]
        m_rest, m_zero = sb("m_rest", [P, TH, 2, UB]), sb("m_zero", [P, TH, 2, UB])
        m_parts = sb("m_parts", [P, TH, 2, M_ROWS, UB], BF16)
        mT_sb = [sb(f"mT{i}", [2 * M_ROWS * UB, T], BF16) for i in range(2)]
        probs = [sb(f"probs{j}", [P, 2, TH, T]) for j in range(NBLK)]
        oT_sb = sb("oT_sb", [P, 4, T])
        o_rec = sb("o_rec", [P, TH, H])
        o_sb = sb("o_sb", [P, TH, D])
        onT = sb("onT", [P, T])
        yn = sb("yn", [P, C4, D])
        xn2 = sb("xn2", [P, C4, D])
        xT = [sb(f"xT{i}", [P, TILE]) for i in range(2)]
        e_sb = sb("e_sb", [P, C4, E])
        score, choice = sb("score", [P, C4, E]), sb("choice", [P, C4, E])
        pair_hi, pair_lo = sb("pair_hi", [P, C4 * GROUPS, 2]), sb("pair_lo", [P, C4 * GROUPS, 2])
        g_top, g_mid, g_low = (sb(f"g_{n}", [P, C4 * GROUPS]) for n in ("top", "mid", "low"))
        g_score = sb("g_score", [P, C4, GROUPS])
        top8 = sb("top8", [P, C4, 8])
        above, need = sb("above", [P, C4, E]), sb("need", [P, C4])
        tied = [sb(f"tied{i}", [P, C4, E // 2 + E]) for i in range(3)]
        picked_g, picked = sb("picked_g", [P, C4, GROUPS]), sb("picked", [P, C4, E])
        w_sum, comb, c_rest = sb("w_sum", [P, C4]), sb("comb", [P, C4, E]), sb("c_rest", [P, C4, E])
        c_parts = sb("c_parts", [P, C4, 3, E], BF16)
        cT = [sb(f"cT{i}", [3 * E, TILE], BF16) for i in range(2)]
        r_sb = [sb(f"r{i}", [P, TILE]) for i in range(2)]
        r2_sb = [sb(f"rr{i}", [P, TILE]) for i in range(2)]
        h_sb = [sb(f"h{i}", [P, TILE]) for i in range(HRING)]
        fT_sb = sb("fT_sb", [P, TILE])
        fn = sb("fn", [P, C4, D])
        ot = [sb(f"ot{i}", [P, C4, D]) for i in range(2)]

        pS1 = [ps(f"pS1_{i}", [P, TILE]) for i in range(2)]
        pS2 = [ps(f"pS2_{i}", [P, 2, TH, T]) for i in range(2)]
        pO = ps("pO", [P, 2, T])
        pM = ps("pM", [P, TILE])
        pMb = pM[:, :].bitcast(BF16)
        pU = [pS1[i][:, :] for i in range(2)]
        pC = [pS2[0][:, i].rearrange("p a b -> p (a b)") for i in range(2)]
        pF = [pS2[1][:, i].rearrange("p a b -> p (a b)") for i in range(2)]
        pN = pO[:, :, :].rearrange("p a b -> p (a b)")

        xq_loaded = [sem(f"xq_loaded{i}") for i in range(2)]
        wa_loaded = sem("wa_loaded")
        wb_loaded = sem("wb_loaded")
        preset = sem("preset")
        ln1_done = sem("ln1_done")
        ln1_link = sem("ln1_link")
        xn_done = sem("xn_done")
        xnT_done = sem("xnT_done")
        xnT_kept = sem("xnT_kept")
        qk_done = sem("qk_done")
        part1_done = sem("part1_done")
        rest_done = sem("rest_done")
        part2_done = sem("part2_done")
        part3_done = sem("part3_done")
        scratch_done = [sem(f"scratch_done{i}") for i in range(2)]
        packed = [sem(f"packed{i}") for i in range(RING)]
        v_done = sem("v_done")
        v_kept = sem("v_kept")
        s1_done = sem("s1_done")
        max_done = sem("max_done")
        mparts_done = sem("mparts_done")
        mparts_link = sem("mparts_link")
        mT_done = sem("mT_done")
        mT_kept = sem("mT_kept")
        m_packed = [sem(f"m_packed{i}") for i in range(RING)]
        s2_done = sem("s2_done")
        exp_done = sem("exp_done")
        pv_done = sem("pv_done")
        oT_kept = sem("oT_kept")
        o_done = sem("o_done")
        rec_done = sem("rec_done")
        o_kept = sem("o_kept")
        onT_done = sem("onT_done")
        onT_kept = sem("onT_kept")
        y_done = sem("y_done")
        y_kept = sem("y_kept")
        ln2_link, ln3_link, ln4_link, rt_link = (sem(n) for n in ("ln2_link", "ln3_link", "ln4_link", "rt_link"))
        ln2_done = sem("ln2_done")
        yn_done = sem("yn_done")
        x1_done = sem("x1_done")
        ln3_done = sem("ln3_done")
        xn2_done = sem("xn2_done")
        x2T_done = sem("x2T_done")
        xT_kept = sem("xT_kept")
        logit_done = sem("logit_done")
        e_done = sem("e_done")
        cparts_done = sem("cparts_done")
        cT_done = sem("cT_done")
        cT_kept = sem("cT_kept")
        up_done = sem("up_done")
        relu_done = sem("relu_done")
        sq_done = sem("sq_done")
        spread_done = sem("spread_done")
        h_done = sem("h_done")
        down_done = sem("down_done")
        fT_kept = sem("fT_kept")
        f_done = sem("f_done")
        ln4_done = sem("ln4_done")
        fn_done = sem("fn_done")
        ot_done = sem("ot_done")
        stored = [sem(f"stored{i}") for i in range(2)]

        N_WA, N_WB = 12, 10
        Y_ALL = NB

        block = ctx.enter_context(nc.Block())

        @block.sync
        def _(sp):
            xd = x.rearrange("(n p) d -> p n d", p=P)
            sp.dma_start(xbig[:, 0:4], xd[:, 0:4]).then_inc(xq_loaded[0], 16)
            sp.dma_start(wq_sb[:, :], wq).then_inc(wa_loaded, 16)
            sp.dma_start(wk_sb[:, :], wk).then_inc(wa_loaded, 16)
            sp.dma_start(idf[:, :], ident_f).then_inc(wa_loaded, 16)
            sp.dma_start(bqk_sb[:, 0:1], bq.unsqueeze(1)).then_inc(wa_loaded, 16)
            sp.dma_start(bqk_sb[:, 1:2], bk.unsqueeze(1)).then_inc(wa_loaded, 16)
            sp.dma_start(wv_sb[:, :], wv).then_inc(wa_loaded, 16)
            for th in range(TH):
                sp.dma_start(bv_sb[:, th], bv.unsqueeze(0).to_broadcast((P, D))).then_inc(wa_loaded, 16)
            sp.dma_start(xbig[:, 4:NT], xd[:, 4:NT]).then_inc(xq_loaded[1], 16)
            sp.dma_start(idb[:, :], ident_b).then_inc(wa_loaded, 16)
            sp.dma_start(wo_sb[:, :], wo).then_inc(wa_loaded, 16)
            for th in range(TH):
                sp.dma_start(bo_sb[:, th], bo.unsqueeze(0).to_broadcast((P, D))).then_inc(wa_loaded, 16)

            def write_parts(b, par):
                sp.wait_ge(part3_done, b + 1)
                for parts, which, scratch in ((q_parts, Q_PARTS, q_scratch), (k_parts, K_PARTS, k_scratch)):
                    s = 0
                    while s < SLOTS:
                        n = 1
                        step = which[s + 1] - which[s] if s + 1 < SLOTS else 0
                        while s + n < SLOTS and step in (0, 1) and which[s + n] - which[s + n - 1] == step:
                            n += 1
                        dst = scratch[b, s:s + n].rearrange("s u d j t -> (u d j) s t")
                        src = (parts[:, which[s]:which[s] + n, :] if n > 1 and step
                               else parts[:, which[s]:which[s] + 1, :].to_broadcast((P, n, T)))
                        sp.dma_start(dst, src).then_inc(scratch_done[par], 16)
                        s += n

            def load_unit(b, half, slot, par, turn):
                sp.wait_ge(scratch_done[par], 6 * 16 * (turn + 1))
                for dst, scratch in ((qp[slot], q_scratch), (kp[slot], k_scratch)):
                    for hh in range(2):
                        sp.dma_start(dst[HR * hh:HR * hh + QK_ROWS, :, :],
                                     scratch[b, :, 2 * half + hh].rearrange("s d j t -> s d (j t)"),
                                     ).then_inc(packed[slot], 16)

            def load_max(u, slot):
                sp.wait_ge(mT_kept, u + 1)
                for hh in range(2):
                    n = M_ROWS * UB
                    sp.dma_start(qp[slot][HR * hh + QK_ROWS:HR * hh + QK_ROWS + M_ROWS, :, :],
                                 mT_sb[slot % 2][n * hh:n * (hh + 1), :]).then_inc(m_packed[slot], 16)

            sp.wait_ge(preset, 1)
            write_parts(0, 0)
            load_unit(0, 0, 0, 0, 0)
            load_unit(0, 1, 1, 0, 0)
            write_parts(1, 1)
            load_unit(1, 0, 2, 1, 0)
            load_max(0, 0)
            wb = [(gate_sb[:, :], gate), (up_sb[:, 0:RBLK], up), (up_sb[:, RBLK:FBLK], shup),
                  (down_sb[:, 0:RBLK], down), (down_sb[:, RBLK:FBLK], shdown), (sel_sb[:, :, :], sel)]
            wb += [(ebias_sb[:, c], ebias.unsqueeze(0).to_broadcast((P, E))) for c in range(C4)]
            assert len(wb) == N_WB

            def batch(it, par, proj):
                b = 2 * it + par
                u = 2 * b
                if not (isinstance(it, int) and b == 0):
                    sp.wait_ge(s2_done, UB * u)
                if proj or par == 0:
                    load_unit(b + 1, 1, (2 * par + 3) % RING, 1 - par, it + par)
                load_max(u + 1, (2 * par + 1) % RING)
                if proj:
                    write_parts(b + 2, par)
                    sp.wait_ge(s2_done, UB * (u + 1))
                    load_unit(b + 2, 0, (2 * par + 4) % RING, par, it + 1)
                if proj or par == 0:
                    load_max(u + 2, (2 * par + 2) % RING)

            for par in range(2):
                batch(0, par, True)
            for dst, src in wb:
                sp.dma_start(dst, src).then_inc(wb_loaded, 16)
            with sp.Fori(1, NB // 2 - 1) as it:
                for par in range(2):
                    batch(it, par, True)
            for par in range(2):
                batch(NB // 2 - 1, par, False)

            od = out.rearrange("(n p) d -> n p d", p=P)

            def store(i, par):
                sp.wait_ge(ot_done, i + 1)
                sp.dma_start(od[bass.ds(C4 * i, C4)].rearrange("n p d -> p n d"),
                             ot[par][:, :, :]).then_inc(stored[par], 16)

            with sp.Fori(0, NTILE // 2) as it:
                for par in range(2):
                    store(2 * it + par, par)
            for par in range(2):
                sp.wait_ge(stored[par], 16 * (NTILE // 2))

        @block.gpsimd
        def _(pool):
            nc.gpsimd.memset(m_zero[:, :, :, :], 0.0)
            for i in range(RING):
                nc.gpsimd.memset(kp[i][:, :, :], 1.0)
            for i in range(3):
                nc.gpsimd.memset(tied[i][:, :, :], 0.0)
            for i in range(2):
                nc.gpsimd.memset(vv[i][:, :, :, DK + 1:VC], 0.0)
                ins = nc.gpsimd.memset(vv[i][:, :, :, DK:DK + 1], 1.0)
            ins.then_inc(preset, 1)

            def split_max(u, par):
                pool.wait_ge(max_done, 2 * UB * (u + 1))
                if not (isinstance(u, int) and u == 0):
                    pool.wait_ge(mT_done, u)
                link = Link(pool, mparts_link, 3 * u)
                m = mneg[par]
                zero = m_zero[:, :, :, :]
                link(nc.gpsimd.tensor_tensor(m_parts[:, :, :, 0], m[:, :, :, :], zero, ALU.add))
                link(nc.gpsimd.tensor_tensor(m_rest[:, :, :, :], m[:, :, :, :], m_parts[:, :, :, 0], ALU.subtract))
                link(nc.gpsimd.tensor_tensor(m_parts[:, :, :, 1], m_rest[:, :, :, :], zero, ALU.add))
                nc.gpsimd.tensor_tensor(m_parts[:, :, :, 2], m_rest[:, :, :, :], m_parts[:, :, :, 1],
                                        ALU.subtract).then_inc(mparts_done, 1)

            for u in range(4):
                split_max(u, u % 2)
            with pool.Fori(1, NU // 4) as it:
                for i in range(4):
                    split_max(4 * it + i, i % 2)

            def residual1(i):
                pool.wait_ge(yn_done, i + 1)
                xi = xbig[:, bass.ds(C4 * i, C4), :]
                nc.gpsimd.tensor_tensor(xi, xi, yn[:, :, :], ALU.add).then_inc(x1_done, 1)

            def residual2(i, par, turn):
                pool.wait_ge(fn_done, i + 1)
                if turn is not None:
                    pool.wait_ge(stored[par], 16 * turn)
                nc.gpsimd.tensor_tensor(ot[par][:, :, :], xbig[:, bass.ds(C4 * i, C4), :], fn[:, :, :],
                                        ALU.add).then_inc(ot_done, 1)

            residual1(0)
            residual1(1)
            residual1(2)
            residual2(0, 0, None)
            residual1(3)
            residual2(1, 1, None)
            with pool.Fori(1, NTILE // 2 - 1) as it:
                for par in range(2):
                    residual1(2 * it + par + 2)
                    residual2(2 * it + par, par, it)
            for par in range(2):
                residual2(NTILE - 2 + par, par, NTILE // 2 - 1)

        @block.scalar
        def _(act):
            def normalise(out_, in_, rs, nm):
                return nc.scalar.activation(out_, in_, ACT.Identity, bias=nm, scale=rs)

            def copy(out_, in_):
                return nc.scalar.activation(out_, in_, ACT.Copy)

            def norm_x(b, first):
                act.wait_ge(ln1_done, 1 if first else 2)
                if not (isinstance(b, int) and b == 0):
                    act.wait_ge(xnT_done, b)
                for th in range(TH):
                    t = bass.ds(TH * b + th, 1)
                    ins = normalise(xn[:, th], xbig[:, t, :], rs1[:, t], nm1[:, t])
                ins.then_inc(xn_done, 1)

            def keep_xnT(b, par, first):
                act.wait_ge(xnT_done, b + 1)
                if not first:
                    act.wait_ge(v_done, b - 1)
                copy(xnT[par][:, :], pM[:, 0:T]).then_inc(xnT_kept, 1)

            def part1(b, par, turn, first):
                act.wait_ge(qk_done, b + 1)
                if not first:
                    act.wait_ge(scratch_done[1 - par], 6 * 16 * (turn + par))
                nc.scalar.activation(q_parts[:, 0], pM[:, 0:T], ACT.Identity, bias=bqk_sb[:, 0:1])
                nc.scalar.activation(k_parts[:, 0], pM[:, T:2 * T], ACT.Identity,
                                     bias=bqk_sb[:, 1:2]).then_inc(part1_done, 1)

            def part2(b):
                act.wait_ge(rest_done, b + 1)
                copy(q_parts[:, 1], q_rest[:, :])
                copy(k_parts[:, 1], k_rest[:, :]).then_inc(part2_done, 1)

            def keep_mT(u, slot, turn):
                act.wait_ge(mT_done, u + 1)
                if turn is not None:
                    act.wait_ge(m_packed[(slot - 2) % RING], 2 * 16 * turn)
                copy(mT_sb[slot % 2][:, :], pMb[0:2 * M_ROWS * UB, 0:T]).then_inc(mT_kept, 1)

            def exp(b, j, first):
                act.wait_ge(s2_done, NBLK * b + j + 1)
                if not first:
                    act.wait_ge(pv_done, 4 * (b - 1) + j // 2 + 1)
                nc.scalar.activation(probs[j][:, :, :, :], pS2[j % 2][:, :, :, :], ACT.Exp,
                                     scale=SCALE).then_inc(exp_done, 1)

            def keep_oT(b, half, first):
                act.wait_ge(pv_done, 4 * b + 2 * half + 2)
                if not first:
                    act.wait_ge(o_done, TH * b)
                copy(oT_sb[:, 2 * half:2 * half + 2, :], pO[:, :, :]).then_inc(oT_kept, 1)

            def keep_onT(b, first):
                act.wait_ge(onT_done, b + 1)
                if not first:
                    act.wait_ge(y_done, b)
                copy(onT[:, :], pM[:, 0:T]).then_inc(onT_kept, 1)

            act.wait_ge(wa_loaded, 16 * N_WA)
            act.wait_ge(xq_loaded[0], 16)
            for b in range(2):
                norm_x(b, True)
                keep_xnT(b, b, True)
                part1(b, b, 0, b == 0)
                part2(b)
            keep_mT(0, 0, None)

            def batch(it, par, proj):
                b = 2 * it + par
                start = isinstance(it, int) and it == 0
                first = start and par == 0
                more = proj or par == 0
                if proj:
                    norm_x(b + 2, False)
                exp(b, 0, first)
                if proj:
                    keep_xnT(b + 2, par, False)
                s1 = (2 * par + 1) % RING
                keep_mT(2 * b + 1, s1, None if first else it + (s1 >= 2))
                exp(b, 1, first)
                if not first:
                    keep_oT(b - 1, 1, start and par == 1)
                exp(b, 2, first)
                if proj:
                    part1(b + 2, par, it + 1, False)
                exp(b, 3, first)
                if proj:
                    part2(b + 2)
                exp(b, 4, first)
                if more:
                    s2 = (2 * par + 2) % RING
                    keep_mT(2 * b + 2, s2, it + 1)
                exp(b, 5, first)
                keep_oT(b, 0, first)
                exp(b, 6, first)
                if not first:
                    keep_onT(b - 1, start and par == 1)
                exp(b, 7, first)

            for par in range(2):
                batch(0, par, True)
            with act.Fori(1, NB // 2 - 1) as it:
                for par in range(2):
                    batch(it, par, True)
            for par in range(2):
                batch(NB // 2 - 1, par, False)
            keep_oT(NB - 1, 1, False)
            keep_onT(NB - 1, False)

            def norm_y(i, c, first):
                if c == 0:
                    act.wait_ge(ln2_done, i + 1)
                    if not first:
                        act.wait_ge(x1_done, i)
                for cc in (c, c + 1):
                    ins = normalise(yn[:, cc], ybig[:, bass.ds(C4 * i + cc, 1), :], rs2[:, cc:cc + 1], nm2[:, cc:cc + 1])
                if c:
                    ins.then_inc(yn_done, 1)

            def norm_x1(i, c, first):
                if c == 0:
                    act.wait_ge(ln3_done, i + 1)
                    if not first:
                        act.wait_ge(x2T_done, i)
                for cc in (c, c + 1):
                    ins = normalise(xn2[:, cc], xbig[:, bass.ds(C4 * i + cc, 1), :], rs3[:, cc:cc + 1], nm3[:, cc:cc + 1])
                if c:
                    ins.then_inc(xn2_done, 1)

            def keep_xT(i, par, first):
                act.wait_ge(x2T_done, i + 1)
                if not first:
                    act.wait_ge(up_done, FBLK * (i - 1))
                copy(xT[par][:, :], pM[:, :]).then_inc(xT_kept, 1)

            def exp_logits(i, first):
                act.wait_ge(logit_done, i + 1)
                if not first:
                    act.wait_ge(cparts_done, i)
                nc.scalar.activation(e_sb[:, :, :], pM[:, 0:C4 * E], ACT.Exp, scale=-1.0).then_inc(e_done, 1)

            def keep_cT(i, par, first):
                act.wait_ge(cT_done, i + 1)
                if not first:
                    act.wait_ge(spread_done, RBLK * (i - 1))
                copy(cT[par][:, :], pMb[0:3 * E, 0:TILE]).then_inc(cT_kept, 1)

            def relu_square(i, k, start):
                n = FBLK * i + k
                act.wait_ge(up_done, n + 1)
                nc.scalar.activation(r_sb[k % 2][:, :], pU[k % 2], ACT.Relu).then_inc(relu_done, 1)
                act.wait_ge(relu_done, n + 1)
                if k < RBLK:
                    if not (start and k < 2):
                        act.wait_ge(h_done, RBLK * i + k - 1)
                    dst = r2_sb[k % 2]
                else:
                    act.wait_ge(down_done, n - 2)
                    dst = h_sb[k % HRING]
                nc.scalar.activation(dst[:, :], r_sb[k % 2][:, :], ACT.Square).then_inc(sq_done, 1)

            def keep_fT(i, par, first):
                act.wait_ge(down_done, FBLK * (i + 1))
                if not first:
                    act.wait_ge(f_done, i)
                copy(fT_sb[:, :], pF[par]).then_inc(fT_kept, 1)

            def norm_f(i, c, first):
                if c == 0:
                    act.wait_ge(ln4_done, i + 1)
                    if not first:
                        act.wait_ge(ot_done, i)
                for cc in (c, c + 1):
                    ins = normalise(fn[:, cc], pN[:, D * cc:D * (cc + 1)], rs4[:, cc:cc + 1], nm4[:, cc:cc + 1])
                if c:
                    ins.then_inc(fn_done, 1)

            norm_y(0, 0, True)
            norm_y(0, 2, True)
            norm_x1(0, 0, True)
            norm_x1(0, 2, True)
            keep_xT(0, 0, True)
            exp_logits(0, True)
            keep_cT(0, 0, True)

            def tile(it, par, more):
                i = 2 * it + par
                start = isinstance(it, int) and it == 0
                prev = not (start and par == 0)
                for k in range(FBLK):
                    relu_square(i, k, start and par == 0)
                    if k == 2 and prev:
                        keep_fT(i - 1, 1 - par, start)
                    if more:
                        if k in (2, 3):
                            norm_y(i + 1, 2 * (k - 2), False)
                        if k in (7, 8):
                            norm_x1(i + 1, 2 * (k - 7), False)
                        if k == 9:
                            keep_xT(i + 1, 1 - par, start and par == 0)
                        if k == 10:
                            exp_logits(i + 1, False)
                        if k == 16:
                            keep_cT(i + 1, 1 - par, start and par == 0)
                    if prev and k in (11, 12):
                        norm_f(i - 1, 2 * (k - 11), start)

            for par in range(2):
                tile(0, par, True)
            with act.Fori(1, NTILE // 2 - 1) as it:
                for par in range(2):
                    tile(it, par, True)
            for par in range(2):
                tile(NTILE // 2 - 1, par, par == 0)
            keep_fT(NTILE - 1, 1, False)
            norm_f(NTILE - 1, 0, False)
            norm_f(NTILE - 1, 2, False)

        @block.vector
        def _(dve):
            def norm_stats(link, tiles, rs, nm, before_write=None):
                n = len(tiles)
                for c, src in enumerate(tiles):
                    ins = nc.vector.bn_stats(stats[:, c, :], src)
                link(ins)
                v, t, y0, m, d = (w[:, 0:n] for w in (nw_v, nw_t, nw_i, nw_m, nw_d))
                even, odd = stats[:, 0:n, 0:3], stats[:, 0:n, 3:6]
                nc.vector.tensor_tensor(d, even[:, :, 1], odd[:, :, 1], ALU.subtract)
                nc.vector.tensor_tensor(m, even[:, :, 1], odd[:, :, 1], ALU.add)
                link(nc.vector.tensor_tensor(v, even[:, :, 2], odd[:, :, 2], ALU.add))
                link(nc.vector.scalar_tensor_tensor(out=d, in0=d, scalar=0.25, in1=d, op0=ALU.mult, op1=ALU.mult))
                link(nc.vector.scalar_tensor_tensor(out=v, in0=v, scalar=1.0 / D, in1=d, op0=ALU.mult, op1=ALU.add))
                link(nc.vector.tensor_scalar(v, v, EPS, None, ALU.add))
                link(nc.vector.tensor_scalar(y0, v.bitcast(I32), 1, None, ALU.arith_shift_right))
                if before_write:
                    dve.wait_ge(*before_write)
                link(nc.vector.tensor_scalar(rs.bitcast(I32), y0, -1.0, float(RSQRT_MAGIC), ALU.mult, ALU.add))
                for _ in range(3):
                    link(nc.vector.tensor_tensor(t, rs, rs, ALU.mult))
                    link(nc.vector.scalar_tensor_tensor(out=t, in0=t, scalar=-0.5, in1=v, op0=ALU.mult, op1=ALU.mult))
                    link(nc.vector.scalar_tensor_tensor(out=rs, in0=t, scalar=1.5, in1=rs, op0=ALU.add, op1=ALU.mult))
                return nc.vector.scalar_tensor_tensor(out=nm, in0=m, scalar=-0.5, in1=rs,
                                                      op0=ALU.mult, op1=ALU.mult)

            def rest(b):
                dve.wait_ge(part1_done, b + 1)
                for i, (left, parts) in enumerate(((q_rest, q_parts), (k_rest, k_parts))):
                    ins = nc.vector.scalar_tensor_tensor(out=left[:, :], in0=pM[:, T * i:T * (i + 1)],
                                                         scalar=bqk_sb[:, i:i + 1], in1=parts[:, 0],
                                                         op0=ALU.add, op1=ALU.subtract)
                ins.then_inc(rest_done, 1)

            def part3(b):
                dve.wait_ge(part2_done, b + 1)
                nc.vector.tensor_tensor(q_parts[:, 2], q_rest[:, :], q_parts[:, 1], ALU.subtract)
                nc.vector.tensor_tensor(k_parts[:, 2], k_rest[:, :], k_parts[:, 1], ALU.subtract).then_inc(part3_done, 1)

            def keep_v(b, par, first):
                dve.wait_ge(v_done, b + 1)
                if not first:
                    dve.wait_ge(pv_done, 4 * (b - 1))
                nc.vector.tensor_tensor(vv[par][:, :, :, 0:DK],
                                        pM[:, 0:T].rearrange("p (a h d) -> p a h d", a=TH, h=H),
                                        bv_sb[:, :, :].rearrange("p a (h d) -> p a h d", h=H),
                                        ALU.add).then_inc(v_kept, 1)

            def row_max(u, upar, k, first):
                if k == 0 and not first:
                    dve.wait_ge(mparts_done, u - 1)
                for hh in range(2):
                    dve.wait_ge(s1_done, 2 * (UB * u + k) + hh + 1)
                    nc.vector.tensor_reduce(mneg[upar][:, :, hh, k], pS1[hh][:, :].rearrange("p (a s) -> p a s", a=TH),
                                            AX.X, ALU.max, negate=True).then_inc(max_done, 1)

            def norm_o(b, th, first):
                dve.wait_ge(o_done, TH * b + th + 1)
                o = pM[:, :].rearrange("p (h c) -> p h c", c=VC)
                nc.vector.reciprocal(o_rec[:, th], o[:, :, DK]).then_inc(rec_done, 1)
                dve.wait_ge(rec_done, TH * b + th + 1)
                if not first:
                    dve.wait_ge(onT_done, b)
                nc.vector.tensor_tensor(o_sb[:, th].rearrange("p (h d) -> p h d", h=H), o[:, :, 0:DK],
                                        o_rec[:, th].unsqueeze(2).to_broadcast((P, H, DK)),
                                        ALU.mult).then_inc(o_kept, 1)

            def keep_y(b):
                dve.wait_ge(y_done, b + 1)
                nc.vector.tensor_tensor(ybig[:, bass.ds(TH * b, TH), :],
                                        pM[:, 0:T].rearrange("p (a e) -> p a e", a=TH), bo_sb[:, :, :],
                                        ALU.add).then_inc(y_kept, 1)

            link = Link(dve, ln1_link, 0)
            dve.wait_ge(xq_loaded[0], 16)
            norm_stats(link, [xbig[:, t] for t in range(4)], rs1[:, 0:4], nm1[:, 0:4]).then_inc(ln1_done, 1)
            dve.wait_ge(wa_loaded, 16 * N_WA)
            dve.wait_ge(preset, 1)
            rest(0)
            part3(0)
            keep_v(0, 0, True)
            rest(1)
            part3(1)
            dve.wait_ge(xq_loaded[1], 16)
            norm_stats(link, [xbig[:, t] for t in range(4, NT)], rs1[:, 4:NT], nm1[:, 4:NT]).then_inc(ln1_done, 1)
            for u in range(2):
                for k in range(UB):
                    row_max(u, u, k, True)

            def batch(it, par, proj):
                b = 2 * it + par
                start = isinstance(it, int) and it == 0
                first = start and par == 0
                more = proj or par == 0
                for j in range(NBLK):
                    if j == 3 and proj:
                        rest(b + 2)
                    if j == 4 and proj:
                        part3(b + 2)
                    if more:
                        row_max(2 * b + 2 + j // UB, j // UB, j % UB, False)
                    if j == 3 and more:
                        keep_v(b + 1, 1 - par, first)
                    if j in (4, 5) and not first:
                        norm_o(b - 1, j - 4, start and par == 1)
                    if j == 7 and not first:
                        keep_y(b - 1)

            for par in range(2):
                batch(0, par, True)
            with dve.Fori(1, NB // 2 - 1) as it:
                for par in range(2):
                    batch(it, par, True)
            for par in range(2):
                batch(NB // 2 - 1, par, False)
            norm_o(NB - 1, 0, False)
            norm_o(NB - 1, 1, False)
            keep_y(NB - 1)

            def stats_y(i, first):
                link = Link(dve, ln2_link, LN_LINKS * i)
                if first:
                    dve.wait_ge(y_kept, Y_ALL)
                norm_stats(link, [ybig[:, bass.ds(C4 * i + c, 1), :] for c in range(C4)], rs2[:, :], nm2[:, :],
                           None if first else (yn_done, i)).then_inc(ln2_done, 1)
                assert link.n == LN_LINKS

            def stats_x1(i, first):
                link = Link(dve, ln3_link, LN_LINKS * i)
                dve.wait_ge(x1_done, i + 1)
                norm_stats(link, [xbig[:, bass.ds(C4 * i + c, 1), :] for c in range(C4)], rs3[:, :], nm3[:, :],
                           None if first else (xn2_done, i)).then_inc(ln3_done, 1)
                assert link.n == LN_LINKS

            def stats_f(i, first):
                link = Link(dve, ln4_link, LN_LINKS * i)
                dve.wait_ge(f_done, i + 1)
                norm_stats(link, [pN[:, D * c:D * (c + 1)] for c in range(C4)], rs4[:, :], nm4[:, :],
                           None if first else (fn_done, i)).then_inc(ln4_done, 1)
                assert link.n == LN_LINKS

            def pick(link, values, least, n, want, picked_):
                pad = E // 2
                ab = above[:, :, 0:n]
                flat = lambda i, s=0: tied[i][:, :, pad - s:pad - s + n]
                least = least.to_broadcast((P, C4, n))
                nc.vector.tensor_tensor(ab, values, least, ALU.is_gt)
                link(nc.vector.tensor_tensor(flat(0), values, least, ALU.is_equal))
                link(nc.vector.tensor_reduce(need[:, :], ab, AX.X, ALU.add))
                link(nc.vector.tensor_scalar(need[:, :], need[:, :], -1.0, float(want), ALU.mult, ALU.add))
                src, s = 0, 1
                while s < n:
                    dst = 2 if src == 1 else 1
                    link(nc.vector.tensor_tensor(flat(dst), flat(src), flat(src, s), ALU.add))
                    src, s = dst, 2 * s
                link(nc.vector.tensor_tensor(picked_, flat(src), need[:, :].unsqueeze(2).to_broadcast((P, C4, n)), ALU.is_le))
                link(nc.vector.tensor_tensor(picked_, picked_, flat(0), ALU.mult))
                link(nc.vector.tensor_tensor(picked_, picked_, ab, ALU.add))

            def route_scores(link, i):
                dve.wait_ge(e_done, i + 1)
                link(nc.vector.tensor_scalar(score[:, :, :], e_sb[:, :, :], 1.0, None, ALU.add))
                link(nc.vector.reciprocal(score[:, :, :], score[:, :, :]))
                link(nc.vector.tensor_tensor(choice[:, :, :], score[:, :, :], ebias_sb[:, :, :], ALU.add))
                g = choice[:, :, :].rearrange("p c (g m) -> p (c g) m", g=GROUPS)
                nc.vector.tensor_tensor(pair_hi[:, :, :], g[:, :, 0:2], g[:, :, 2:4], ALU.max)
                link(nc.vector.tensor_tensor(pair_lo[:, :, :], g[:, :, 0:2], g[:, :, 2:4], ALU.min))
                nc.vector.tensor_tensor(g_top[:, :], pair_hi[:, :, 0], pair_hi[:, :, 1], ALU.max)
                nc.vector.tensor_tensor(g_mid[:, :], pair_hi[:, :, 0], pair_hi[:, :, 1], ALU.min)
                link(nc.vector.tensor_tensor(g_low[:, :], pair_lo[:, :, 0], pair_lo[:, :, 1], ALU.max))
                link(nc.vector.tensor_tensor(g_mid[:, :], g_mid[:, :], g_low[:, :], ALU.max))
                link(nc.vector.tensor_tensor(g_score[:, :, :].rearrange("p c g -> p (c g)"), g_top[:, :], g_mid[:, :], ALU.add))

            def route_groups(link):
                for c in range(C4):
                    ins = nc.vector.max(top8[:, c], g_score[:, c])
                link(ins)
                pick(link, g_score[:, :, :], top8[:, :, TOPG - 1:TOPG], GROUPS, TOPG, picked_g[:, :, :])
                g = choice[:, :, :].rearrange("p c (g m) -> p (c g) m", g=GROUPS)
                link(nc.vector.tensor_tensor(g, g, picked_g[:, :, :].rearrange("p c g -> p (c g)").unsqueeze(2)
                                             .to_broadcast((P, C4 * GROUPS, E // GROUPS)), ALU.mult))

            def route_experts(link):
                for c in range(C4):
                    ins = nc.vector.max(top8[:, c], choice[:, c])
                link(ins)
                pick(link, choice[:, :, :], top8[:, :, TOPK - 1:TOPK], E, TOPK, picked[:, :, :])

            def route_weights(link, i, first):
                link(nc.vector.tensor_tensor(comb[:, :, :], score[:, :, :], picked[:, :, :], ALU.mult))
                link(nc.vector.tensor_reduce(w_sum[:, :], comb[:, :, :], AX.X, ALU.add))
                link(nc.vector.tensor_scalar(w_sum[:, :], w_sum[:, :], 1e-20, None, ALU.add))
                link(nc.vector.reciprocal(w_sum[:, :], w_sum[:, :]))
                link(nc.vector.scalar_tensor_tensor(out=comb[:, :, :], in0=comb[:, :, :], scalar=ROUTED_SCALE,
                                                    in1=w_sum[:, :].unsqueeze(2).to_broadcast((P, C4, E)),
                                                    op0=ALU.mult, op1=ALU.mult))
                if not first:
                    dve.wait_ge(cT_done, i)
                link(nc.vector.tensor_copy(c_parts[:, :, 0], comb[:, :, :]))
                link(nc.vector.tensor_tensor(c_rest[:, :, :], comb[:, :, :], c_parts[:, :, 0], ALU.subtract))
                link(nc.vector.tensor_copy(c_parts[:, :, 1], c_rest[:, :, :]))
                nc.vector.tensor_tensor(c_parts[:, :, 2], c_rest[:, :, :], c_parts[:, :, 1],
                                        ALU.subtract).then_inc(cparts_done, 1)
                assert link.n == RT_LINKS, link.n

            def weigh(i, k, par, start):
                dve.wait_ge(sq_done, FBLK * i + k + 1)
                dve.wait_ge(spread_done, RBLK * i + k + 1)
                if not (start and k < HRING):
                    dve.wait_ge(down_done, FBLK * i + k - 2)
                nc.vector.tensor_tensor(h_sb[k % HRING][:, :], pC[k % 2], r2_sb[k % 2][:, :],
                                        ALU.mult).then_inc(h_done, 1)

            dve.wait_ge(wb_loaded, 16 * N_WB)
            stats_y(0, True)
            stats_x1(0, True)
            link = Link(dve, rt_link, 0)
            route_scores(link, 0)
            route_groups(link)
            route_experts(link)
            route_weights(link, 0, True)

            def tile(it, par, more):
                i = 2 * it + par
                start = isinstance(it, int) and it == 0
                prev = not (start and par == 0)
                link = Link(dve, rt_link, RT_LINKS * (i + 1))
                for k in range(RBLK):
                    weigh(i, k, par, start and par == 0)
                    if more:
                        if k == 0:
                            stats_y(i + 1, False)
                        if k == 5:
                            stats_x1(i + 1, False)
                        if k == 10:
                            route_scores(link, i + 1)
                        if k == 11:
                            route_groups(link)
                        if k == 12:
                            route_experts(link)
                        if k == 13:
                            route_weights(link, i + 1, False)
                    if prev and k == 8:
                        stats_f(i - 1, start)

            for par in range(2):
                tile(0, par, True)
            with dve.Fori(1, NTILE // 2 - 1) as it:
                for par in range(2):
                    tile(it, par, True)
            for par in range(2):
                tile(NTILE // 2 - 1, par, par == 0)
            stats_f(NTILE - 1, False)

        @block.tensor
        def _(pe):
            mm, tr = nc.tensor.matmul, nc.tensor.transpose

            def transpose_x(b):
                pe.wait_ge(xn_done, b + 1)
                for th in range(TH):
                    ins = tr(pM[:, P * th:P * (th + 1)], xn[:, th], idf[:, :])
                ins.then_inc(xnT_done, 1)

            def project_qk(b, par):
                pe.wait_ge(xnT_kept, b + 1)
                mm(pM[:, 0:T], wq_sb[:, :], xnT[par][:, :], start=True, stop=True)
                mm(pM[:, T:2 * T], wk_sb[:, :], xnT[par][:, :], start=True, stop=True).then_inc(qk_done, 1)

            def project_v(b, par):
                pe.wait_ge(xnT_kept, b + 1)
                for th in range(TH):
                    ins = mm(pM[:, D * th:D * (th + 1)], xnT[par][:, P * th:P * (th + 1)], wv_sb[:, :],
                             start=True, stop=True)
                ins.then_inc(v_done, 1)

            def scores_by_query(u, slot, turn, k, hh, first):
                if k == 0 and hh == 0:
                    pe.wait_ge(packed[slot], 4 * 16 * (turn + 1))
                if not (first and k == 0):
                    pe.wait_ge(max_done, 2 * (UB * u + k) + hh - 1)
                r = slice(HR * hh, HR * hh + QK_ROWS)
                for th in range(TH):
                    ins = mm(pS1[hh][:, T * th:T * (th + 1)], qp[slot][r, k, P * th:P * (th + 1)],
                             kp[slot][r, k, :], start=True, stop=True)
                ins.then_inc(s1_done, 1)

            def scores_by_key(b, j, slot, turn, hh, first):
                if j % UB == 0 and hh == 0:
                    pe.wait_ge(m_packed[slot], 2 * 16 * (turn + 1))
                if hh == 0 and not (first and j < 2):
                    pe.wait_ge(exp_done, NBLK * b + j - 1)
                r = slice(HR * hh, HR * hh + QK_ROWS + M_ROWS)
                for sh in range(TH):
                    ins = mm(pS2[j % 2][:, hh, sh], kp[slot][r, j % UB, P * sh:P * (sh + 1)],
                             qp[slot][r, j % UB, :], start=True, stop=True)
                if hh == 1:
                    ins.then_inc(s2_done, 1)

            def outputs(b, g, par, first):
                pe.wait_ge(exp_done, NBLK * b + 2 * g + 2)
                if g == 0:
                    pe.wait_ge(v_kept, b + 1)
                if g % 2 == 0 and not (first and g == 0):
                    pe.wait_ge(oT_kept, 2 * b + g // 2)
                for sh in range(TH):
                    for h in range(4):
                        ins = mm(pO[VC * h:VC * (h + 1), g % 2], vv[par][:, sh, 4 * g + h, :],
                                 probs[2 * g + h // 2][:, h % 2, sh, :], start=sh == 0, stop=sh == TH - 1)
                ins.then_inc(pv_done, 1)

            def transpose_max(u):
                pe.wait_ge(mparts_done, u + 1)
                for th in range(TH):
                    ins = tr(pMb[0:2 * M_ROWS * UB, P * th:P * (th + 1)],
                             m_parts[:, th].rearrange("p a b c -> p (a b c)"), idb[:, :])
                ins.then_inc(mT_done, 1)

            def transpose_o(b, th):
                pe.wait_ge(oT_kept, 2 * b + 2)
                for g in range(4):
                    ins = tr(pM[:, P * g:P * (g + 1)], oT_sb[:, g, P * th:P * (th + 1)], idf[:, :])
                ins.then_inc(o_done, 1)

            def transpose_on(b):
                pe.wait_ge(o_kept, TH * (b + 1))
                for th in range(TH):
                    ins = tr(pM[:, P * th:P * (th + 1)], o_sb[:, th], idf[:, :])
                ins.then_inc(onT_done, 1)

            def project_y(b):
                pe.wait_ge(onT_kept, b + 1)
                for th in range(TH):
                    ins = mm(pM[:, D * th:D * (th + 1)], onT[:, P * th:P * (th + 1)], wo_sb[:, :],
                             start=True, stop=True)
                ins.then_inc(y_done, 1)

            pe.wait_ge(wa_loaded, 16 * N_WA)
            transpose_x(0)
            project_qk(0, 0)
            pe.wait_ge(rest_done, 1)
            project_v(0, 0)
            pe.wait_ge(v_kept, 1)
            transpose_x(1)
            project_qk(1, 1)
            for u in range(2):
                for k in range(UB):
                    for hh in range(2):
                        scores_by_query(u, u, 0, k, hh, u == 0)
                if u == 0:
                    pe.wait_ge(rest_done, 2)
                    transpose_max(0)

            def batch(it, par, proj):
                b = 2 * it + par
                start = isinstance(it, int) and it == 0
                first = start and par == 0
                more = proj or par == 0
                second = start and par == 1
                for j in range(NBLK):
                    half, k = j // UB, j % UB
                    ahead = (2 * par + 2 + half) % RING
                    turn = it + (2 * par + 2 + half) // RING
                    if j == 1:
                        if proj:
                            pe.wait_ge(xnT_kept, b + 3)
                        else:
                            pe.wait_ge(mT_kept, 2 * b + 1)
                            pe.wait_ge(y_kept, b - 1)
                        transpose_max(2 * b + 1)
                    if j == 5 and more:
                        pe.wait_ge(v_kept, b + 2)
                        if not first:
                            pe.wait_ge(o_kept, TH * (b - 1) + 1)
                        transpose_max(2 * b + 2)
                    for hh in range(2):
                        if more:
                            scores_by_query(2 * b + 2 + half, ahead, turn, k, hh, False)
                        scores_by_key(b, j, (2 * par + half) % RING, it, hh, first)
                    if j == 0 and proj:
                        pe.wait_ge(mT_kept, 2 * b + 1)
                        if not first and not second:
                            pe.wait_ge(y_kept, b - 1)
                        transpose_x(b + 2)
                    if j == 1 and not first:
                        outputs(b - 1, 3, 1 - par, False)
                    if j == 2 and proj:
                        pe.wait_ge(mT_kept, 2 * b + 2)
                        project_qk(b + 2, par)
                    if j == 3:
                        if more:
                            pe.wait_ge(mT_kept, 2 * b + 2)
                            if proj:
                                pe.wait_ge(rest_done, b + 3)
                            project_v(b + 1, 1 - par)
                        outputs(b, 0, par, first)
                    if j == 4 and not first:
                        pe.wait_ge(mT_kept, 2 * b + 2)
                        if more:
                            pe.wait_ge(v_kept, b + 2)
                        transpose_o(b - 1, 0)
                    if j == 5:
                        if not first:
                            pe.wait_ge(o_kept, TH * (b - 1) + 1)
                            if more:
                                pe.wait_ge(mT_kept, 2 * b + 3)
                            transpose_o(b - 1, 1)
                        outputs(b, 1, par, first)
                    if j == 6 and not first:
                        transpose_on(b - 1)
                    if j == 7:
                        if not first:
                            project_y(b - 1)
                        outputs(b, 2, par, first)

            for par in range(2):
                batch(0, par, True)
            with pe.Fori(1, NB // 2 - 1) as it:
                for par in range(2):
                    batch(it, par, True)
            for par in range(2):
                batch(NB // 2 - 1, par, False)
            outputs(NB - 1, 3, 1, False)
            pe.wait_ge(y_kept, NB - 1)
            transpose_o(NB - 1, 0)
            pe.wait_ge(o_kept, TH * (NB - 1) + 1)
            transpose_o(NB - 1, 1)
            transpose_on(NB - 1)
            project_y(NB - 1)

            def transpose_x1(i, first):
                pe.wait_ge(xn2_done, i + 1)
                if not first:
                    pe.wait_ge(cT_kept, i)
                for c in range(C4):
                    ins = tr(pM[:, P * c:P * (c + 1)], xn2[:, c], idf[:, :])
                ins.then_inc(x2T_done, 1)

            def logits(i, par):
                pe.wait_ge(xT_kept, i + 1)
                for c in range(C4):
                    ins = mm(pM[:, E * c:E * (c + 1)], xT[par][:, P * c:P * (c + 1)], gate_sb[:, :],
                             start=True, stop=True)
                ins.then_inc(logit_done, 1)

            def transpose_c(i):
                pe.wait_ge(cparts_done, i + 1)
                for c in range(C4):
                    ins = tr(pMb[0:3 * E, P * c:P * (c + 1)], c_parts[:, c].rearrange("p a e -> p (a e)"), idb[:, :])
                ins.then_inc(cT_done, 1)

            def up_block(i, k, par, start):
                if not (start and k < 2):
                    pe.wait_ge(relu_done, FBLK * i + k - 1)
                mm(pU[k % 2], up_sb[:, k], xT[par][:, :], start=True, stop=True).then_inc(up_done, 1)
                if k < RBLK:
                    if k == 0:
                        pe.wait_ge(cT_kept, i + 1)
                    if not (start and k < 2):
                        pe.wait_ge(h_done, RBLK * i + k - 1)
                    mm(pC[k % 2], sel_sb[:, k], cT[par][:, :], start=True, stop=True).then_inc(spread_done, 1)

            def down_block(i, k, par, start):
                if k < RBLK:
                    pe.wait_ge(h_done, RBLK * i + k + 1)
                else:
                    pe.wait_ge(sq_done, FBLK * i + k + 1)
                if k == 0 and not start:
                    pe.wait_ge(fT_kept, i - 1)
                mm(pF[par], down_sb[:, k], h_sb[k % HRING][:, :], start=k == 0,
                   stop=k == FBLK - 1).then_inc(down_done, 1)

            def transpose_f(i, first):
                pe.wait_ge(fT_kept, i + 1)
                if not first:
                    pe.wait_ge(fn_done, i)
                for c in range(C4):
                    ins = tr(pN[:, P * c:P * (c + 1)], fT_sb[:, P * c:P * (c + 1)], idf[:, :])
                ins.then_inc(f_done, 1)

            pe.wait_ge(y_kept, Y_ALL)
            pe.wait_ge(max_done, H * NB)
            pe.wait_ge(exp_done, NBLK * NB)
            pe.wait_ge(oT_kept, 2 * NB)
            pe.wait_ge(wb_loaded, 16 * N_WB)
            transpose_x1(0, True)
            logits(0, 0)
            transpose_c(0)

            def tile(it, par, more):
                i = 2 * it + par
                start = isinstance(it, int) and it == 0
                prev = not (start and par == 0)
                for k in range(FBLK):
                    up_block(i, k, par, start and par == 0)
                    if k >= LAG:
                        down_block(i, k - LAG, par, start)
                    elif prev:
                        down_block(i - 1, FBLK - LAG + k, 1 - par, start)
                    if k == 4 and prev:
                        transpose_f(i - 1, start)
                    if more:
                        if k == 9:
                            transpose_x1(i + 1, False)
                        if k == 10:
                            logits(i + 1, 1 - par)
                        if k == 15:
                            transpose_c(i + 1)

            for par in range(2):
                tile(0, par, True)
            with pe.Fori(1, NTILE // 2 - 1) as it:
                for par in range(2):
                    tile(it, par, True)
            for par in range(2):
                tile(NTILE // 2 - 1, par, par == 0)
            for k in range(FBLK - LAG, FBLK):
                down_block(NTILE - 1, k, 1, False)
            transpose_f(NTILE - 1, False)


def kernel(**inputs):
    import ml_dtypes
    import concourse.bacc as bacc
    from concourse.bass_utils import run_bass_kernel_spmd

    a = {k: np.asarray(v) for k, v in inputs.items()}
    order = lambda w: w.reshape((2, UB, 2, DK) + w.shape[1:]).transpose(
        (0, 2, 3, 1) + tuple(range(4, 3 + w.ndim))).reshape(w.shape)
    names = ["x", "wq", "wk", "wv", "wo", "bq", "bk", "bv", "bo", "gate", "ebias", "up", "shup", "down", "shdown",
             "ident_f", "ident_b", "sel"]
    sel = np.zeros((3, E, RBLK, P), ml_dtypes.bfloat16)
    for e in range(E):
        blk, at = divmod(e * EI, P)
        sel[:, e, blk, at:at + EI] = 1
    arrays = {
        "x": a["L0_attn_x"].reshape(NB * T, D),
        "wq": order(a["L0_attn_w_q"]).T,
        "wk": order(a["L0_attn_w_k"]).T,
        "wv": a["L0_attn_w_v"].T,
        "wo": a["L0_attn_w_o"].T,
        "bq": order(a["L0_attn_b_q"]),
        "bk": order(a["L0_attn_b_k"]),
        "bv": a["L0_attn_b_v"],
        "bo": a["L0_attn_b_o"],
        "gate": a["L0_ffn_gate_w"].T,
        "ebias": a["L0_ffn_e_bias"],
        "up": a["L0_ffn_up_w"].reshape(RBLK, P, D).transpose(2, 0, 1),
        "shup": a["L0_ffn_shared_up_w"].reshape(SI // P, P, D).transpose(2, 0, 1),
        "down": a["L0_ffn_down_w"].reshape(RBLK, P // EI, D, EI).transpose(1, 3, 0, 2).reshape(P, RBLK, D),
        "shdown": a["L0_ffn_shared_down_w"].reshape(D, SI // P, P).transpose(2, 1, 0),
        "ident_f": np.eye(P, dtype=np.float32),
        "ident_b": np.eye(P, dtype=ml_dtypes.bfloat16),
        "sel": sel.reshape(3 * E, RBLK, P),
    }
    nc = bacc.Bacc("TRN2", target_bir_lowering=False, num_devices=1)
    nc.disable_value_cache = True
    args, maps = [], {}
    for name in names:
        v = np.ascontiguousarray(arrays[name])
        maps[f"in_{name}"] = v
        args.append(nc.dram_tensor(f"in_{name}", v.shape, mybir.dt.from_np(v.dtype), kind="ExternalInput").ap())
    args.append(nc.dram_tensor("out_x", (NB * T, D), F32, kind="ExternalOutput").ap())
    block_kernel(nc, *args)
    r = run_bass_kernel_spmd(nc, [maps], core_ids=[0])
    return r.results[0]["out_x"].reshape(NB, T, D)
```

```python
from contextlib import ExitStack

import numpy as np

import concourse.bass as bass
from concourse import mybir

F32 = mybir.dt.float32
BF16 = mybir.dt.bfloat16
I32 = mybir.dt.int32
ALU = mybir.AluOpType
ACT = mybir.ActivationFunctionType
AX = mybir.AxisListType

P = 128
NB, T, D = 16, 256, 128
H, DK = 16, 8
TH = T // P
NT = NB * TH
NBLK = H // 2
UB = NBLK // 2
NU = 2 * NB
SLOTS = 6
Q_PARTS = (0, 0, 0, 1, 1, 2)
K_PARTS = (0, 1, 2, 0, 1, 0)
QK_ROWS = SLOTS * DK
M_ROWS = 3
DIFF_ROWS = 2 * QK_ROWS + 2 * M_ROWS
RING = 4
S2_RING = 3
SCALE = float(DK) ** -0.5
VC = 32

E, EI, GROUPS, TOPG, TOPK = 32, 64, 8, 4, 6
ROUTED_SCALE = 2.5
SI = 256
TILE = 512
NTILE = NB * T // TILE
C4 = TILE // P
RBLK = E * EI // P
FBLK = RBLK + SI // P
HRING = 4
AHEAD = 3
FIRST = 2 * AHEAD
SECOND = 4 * AHEAD
PREP = (6, 9)
LAG = 3
EPS = 1e-5
RSQRT_MAGIC = 0x5F3759DF
LN_LINKS = 17
RT_LINKS = 38


class Link:

    def __init__(self, eng, sem, base):
        self.eng, self.sem, self.base, self.n = eng, sem, base, 0

    def __call__(self, instruction):
        self.n += 1
        instruction.then_inc(self.sem, 1)
        self.eng.wait_ge(self.sem, self.base + self.n)


def block_kernel(nc, x, wq, wk, wv, wo, bq, bk, bv, bo, gate, ebias, up, shup, down, shdown,
                 ident_f, ident_b, sel, out):
    with ExitStack() as ctx:
        def sb(name, shape, dt=F32):
            return ctx.enter_context(nc.sbuf_tensor(name, shape, dt))

        def ps(name, shape):
            return ctx.enter_context(nc.psum_tensor(name, shape, F32))

        def sem(name):
            return ctx.enter_context(nc.semaphore(name))

        q_scratch = nc.dram_tensor("q_scratch", (NB, SLOTS, 4, DK, UB, T), BF16).ap()
        k_scratch = nc.dram_tensor("k_scratch", (NB, SLOTS, 4, DK, UB, T), BF16).ap()

        xbig = sb("xbig", [P, NT, D])
        ybig = sb("ybig", [P, NT, D])
        wq_sb, wk_sb = sb("wq_sb", [P, D]), sb("wk_sb", [P, D])
        wv_sb, wo_sb = sb("wv_sb", [P, D]), sb("wo_sb", [P, D])
        bqk_sb = sb("bqk_sb", [P, 2])
        bv_sb, bo_sb = sb("bv_sb", [P, TH, D]), sb("bo_sb", [P, TH, D])
        gate_sb = sb("gate_sb", [P, E])
        ebias_sb = sb("ebias_sb", [P, C4, E])
        up_sb = sb("up_sb", [P, FBLK, P])
        down_sb = sb("down_sb", [P, FBLK, D])
        idf, idb = sb("idf", [P, P]), sb("idb", [P, P], BF16)
        sel_sb = sb("sel_sb", [3 * E, RBLK, P], BF16)
        stats, stats2, stats3, stats4 = (sb(n, [P, c, 6]) for n, c in (
            ("stats", NT), ("stats2", C4), ("stats3", C4), ("stats4", C4)))
        rs1, nm1 = sb("rs1", [P, NT]), sb("nm1", [P, NT])
        rs2, nm2 = sb("rs2", [P, C4]), sb("nm2", [P, C4])
        rs3, nm3 = sb("rs3", [P, C4]), sb("nm3", [P, C4])
        rs4, nm4 = sb("rs4", [P, C4]), sb("nm4", [P, C4])
        nw_v, nw_t, nw_m, nw_d, nw_h = (sb(f"nw_{n}", [P, NT]) for n in "vtmdh")
        work2, work3, work4 = ([sb(f"work{k}_{n}", [P, C4]) for n in "vtmdh"] for k in (2, 3, 4))
        tiny = sb("tiny", [P, 2])
        xn = sb("xn", [P, TH, D])
        xnT = [sb(f"xnT{i}", [P, T]) for i in range(2)]
        q_parts = [sb(f"q_parts{i}", [P, 3, T], BF16) for i in range(2)]
        k_parts = [sb(f"k_parts{i}", [P, 3, T], BF16) for i in range(2)]
        q_rest, k_rest = sb("q_rest", [P, T]), sb("k_rest", [P, T])
        qp = [sb(f"qp{i}", [P, 2, UB, T], BF16) for i in range(RING)]
        kp = [sb(f"kp{i}", [P, UB, T], BF16) for i in range(RING)]
        vv = [sb(f"vv{i}", [P, TH, H, VC]) for i in range(2)]
        mneg = [sb(f"mneg{i}", [P, TH, 2, UB]) for i in range(2)]
        m_rest, m_zero = sb("m_rest", [P, TH, 2, UB]), sb("m_zero", [P, TH, 2, UB])
        m_parts = sb("m_parts", [P, TH, 2, M_ROWS, UB], BF16)
        mT_sb = [sb(f"mT{i}", [2 * M_ROWS * UB, T], BF16) for i in range(2)]
        probs = [sb(f"probs{j}", [P, TH, 2, T]) for j in range(NBLK)]
        oT_sb = sb("oT_sb", [P, 4, T])
        o_rec = sb("o_rec", [P, TH, H])
        o_sb = sb("o_sb", [P, TH, D])
        onT = sb("onT", [P, T])
        yn = sb("yn", [P, C4, D])
        xn2 = sb("xn2", [P, C4, D])
        xT = [sb(f"xT{i}", [P, TILE]) for i in range(2)]
        e_sb = sb("e_sb", [P, C4, E])
        score, choice = sb("score", [P, C4, E]), sb("choice", [P, C4, E])
        pair_hi, pair_lo = sb("pair_hi", [P, C4 * GROUPS, 2]), sb("pair_lo", [P, C4 * GROUPS, 2])
        g_top, g_mid, g_low = (sb(f"g_{n}", [P, C4 * GROUPS]) for n in ("top", "mid", "low"))
        g_score = sb("g_score", [P, C4, GROUPS])
        top8 = sb("top8", [P, C4, 8])
        above, need = sb("above", [P, C4, E]), sb("need", [P, C4])
        tied = [sb(f"tied{i}", [P, C4, E // 2 + E]) for i in range(3)]
        picked_g, picked = sb("picked_g", [P, C4, GROUPS]), sb("picked", [P, C4, E])
        w_sum, comb, c_rest = sb("w_sum", [P, C4]), sb("comb", [P, C4, E]), sb("c_rest", [P, C4, E])
        c_parts = sb("c_parts", [P, C4, 3, E], BF16)
        cT = [sb(f"cT{i}", [3 * E, TILE], BF16) for i in range(2)]
        r_sb = [sb(f"r{i}", [P, TILE]) for i in range(2)]
        r2_sb = [sb(f"rr{i}", [P, TILE]) for i in range(2)]
        h_sb = [sb(f"h{i}", [P, TILE]) for i in range(HRING)]
        fT_sb = sb("fT_sb", [P, TILE])
        fn = sb("fn", [P, C4, D])
        ot = [sb(f"ot{i}", [P, C4, D]) for i in range(2)]

        pS1 = [ps(f"pS1_{i}", [P, TILE]) for i in range(2)]
        pS2 = [ps(f"pS2_{i}", [P, 2, T]) for i in range(S2_RING)]
        pO = ps("pO", [P, 2, T])
        pX, pY = ps("pX", [P, TILE]), ps("pY", [P, TILE])
        pXb = pX[:, :].bitcast(BF16)
        pU = [pS1[i][:, :] for i in range(2)]
        pC = [pS2[i][:, :, :].rearrange("p a b -> p (a b)") for i in range(2)]
        pF = [pS2[2][:, :, :].rearrange("p a b -> p (a b)"), pY[:, :]]
        pN = pO[:, :, :].rearrange("p a b -> p (a b)")

        xq_loaded = [sem(f"xq_loaded{i}") for i in range(2)]
        wqk_loaded = sem("wqk_loaded")
        wa_loaded = sem("wa_loaded")
        wb_loaded = sem("wb_loaded")
        tiny_set = sem("tiny_set")
        preset = sem("preset")
        ones_set = sem("ones_set")
        ln1_done = sem("ln1_done")
        ln1_stats = sem("ln1_stats")
        ln1_rest_done = sem("ln1_rest_done")
        ln1_rest_link = sem("ln1_rest_link")
        ln1_link = sem("ln1_link")
        xn_done = sem("xn_done")
        xnT_done = sem("xnT_done")
        xnT_kept = sem("xnT_kept")
        qk_done = sem("qk_done")
        part1_done = sem("part1_done")
        rest_done = sem("rest_done")
        part2_done = sem("part2_done")
        part3_done = sem("part3_done")
        scratch_done = [sem(f"scratch_done{i}") for i in range(2)]
        packed = [sem(f"packed{i}") for i in range(RING)]
        v_done = sem("v_done")
        v_kept = sem("v_kept")
        s1_done = sem("s1_done")
        max_done = sem("max_done")
        mparts_done = sem("mparts_done")
        mparts_link = sem("mparts_link")
        mT_done = sem("mT_done")
        mT_kept = sem("mT_kept")
        m_packed = [sem(f"m_packed{i}") for i in range(RING)]
        s2_done = sem("s2_done")
        exp_done = sem("exp_done")
        pv_done = sem("pv_done")
        oT_kept = sem("oT_kept")
        o_done = sem("o_done")
        rec_done = sem("rec_done")
        o_kept = sem("o_kept")
        onT_done = sem("onT_done")
        onT_kept = sem("onT_kept")
        y_done = sem("y_done")
        y_kept = sem("y_kept")
        ln2_link, ln3_link, ln4_link, rt_link = (sem(n) for n in ("ln2_link", "ln3_link", "ln4_link", "rt_link"))
        y_stats, x1_stats, f_stats = (sem(n) for n in ("y_stats", "x1_stats", "f_stats"))
        ln2_done = sem("ln2_done")
        yn_done = sem("yn_done")
        x1_done = sem("x1_done")
        ln3_done = sem("ln3_done")
        xn2_done = sem("xn2_done")
        x2T_done = sem("x2T_done")
        xT_kept = sem("xT_kept")
        logit_done = sem("logit_done")
        e_done = sem("e_done")
        cparts_done = sem("cparts_done")
        cT_done = sem("cT_done")
        cT_kept = sem("cT_kept")
        up_done = sem("up_done")
        relu_done = sem("relu_done")
        sq_done = sem("sq_done")
        spread_done = sem("spread_done")
        h_done = sem("h_done")
        down_done = sem("down_done")
        fT_kept = sem("fT_kept")
        f_done = sem("f_done")
        ln4_done = sem("ln4_done")
        fn_done = sem("fn_done")
        ot_done = sem("ot_done")
        stored = [sem(f"stored{i}") for i in range(2)]

        N_WQK, N_WA, N_WB = 5, 7, 10
        N_PARTS = 16 * 6
        Y_ALL = NB

        block = ctx.enter_context(nc.Block())

        def norm_chain(eng, wait, link, st, work, rs, nm, before_write=None):
            v, t, m, d, half = work
            even, odd = st[:, :, 0:3], st[:, :, 3:6]
            eng.tensor_tensor(d, even[:, :, 1], odd[:, :, 1], ALU.subtract)
            eng.tensor_tensor(m, even[:, :, 1], odd[:, :, 1], ALU.add)
            link(eng.tensor_tensor(v, even[:, :, 2], odd[:, :, 2], ALU.add))
            eng.tensor_tensor(d, d, d, ALU.mult)
            eng.tensor_scalar(m, m, -0.5, None, ALU.mult)
            link(eng.tensor_scalar(v, v, 1.0 / D, EPS, ALU.mult, ALU.add))
            link(eng.tensor_scalar(d, d, 0.25, None, ALU.mult))
            link(eng.tensor_tensor(v, v, d, ALU.add))
            if before_write:
                wait(*before_write)
            eng.tensor_scalar(half, v, -0.5, None, ALU.mult)
            link(eng.tensor_scalar(rs.bitcast(I32), v.bitcast(I32), -0.5, float(RSQRT_MAGIC), ALU.mult, ALU.add))
            for _ in range(3):
                link(eng.tensor_tensor(t, rs, rs, ALU.mult))
                link(eng.tensor_tensor(t, t, half, ALU.mult))
                link(eng.tensor_scalar(t, t, 1.5, None, ALU.add))
                link(eng.tensor_tensor(rs, rs, t, ALU.mult))
            return eng.tensor_tensor(nm, m, rs, ALU.mult)

        @block.sync
        def _(sp):
            xd = x.rearrange("(n p) d -> p n d", p=P)
            sp.dma_start(xbig[:, 0:FIRST], xd[:, 0:FIRST]).then_inc(xq_loaded[0], 16)
            sp.dma_start(idf[:, :], ident_f).then_inc(wqk_loaded, 16)
            sp.dma_start(wq_sb[:, :], wq).then_inc(wqk_loaded, 16)
            sp.dma_start(wk_sb[:, :], wk).then_inc(wqk_loaded, 16)
            sp.dma_start(bqk_sb[:, 0:1], bq.unsqueeze(1)).then_inc(wqk_loaded, 16)
            sp.dma_start(bqk_sb[:, 1:2], bk.unsqueeze(1)).then_inc(wqk_loaded, 16)
            sp.dma_start(wv_sb[:, :], wv).then_inc(wa_loaded, 16)
            for th in range(TH):
                sp.dma_start(bv_sb[:, th], bv.unsqueeze(0).to_broadcast((P, D))).then_inc(wa_loaded, 16)
            sp.dma_start(idb[:, :], ident_b).then_inc(wa_loaded, 16)
            sp.dma_start(wo_sb[:, :], wo).then_inc(wa_loaded, 16)
            for th in range(TH):
                sp.dma_start(bo_sb[:, th], bo.unsqueeze(0).to_broadcast((P, D))).then_inc(wa_loaded, 16)
            sp.dma_start(xbig[:, FIRST:NT], xd[:, FIRST:NT]).then_inc(xq_loaded[1], 16)

            def write_parts(b):
                sp.wait_ge(part3_done, b + 1)
                for parts, which, scratch in ((q_parts[b % 2], Q_PARTS, q_scratch), (k_parts[b % 2], K_PARTS, k_scratch)):
                    s = 0
                    while s < SLOTS:
                        n = 1
                        step = which[s + 1] - which[s] if s + 1 < SLOTS else 0
                        while s + n < SLOTS and step in (0, 1) and which[s + n] - which[s + n - 1] == step:
                            n += 1
                        dst = scratch[b, s:s + n].rearrange("s u d j t -> (u d j) s t")
                        src = (parts[:, which[s]:which[s] + n, :] if n > 1 and step
                               else parts[:, which[s]:which[s] + 1, :].to_broadcast((P, n, T)))
                        sp.dma_start(dst, src).then_inc(scratch_done[b % 2], 16)
                        s += n

            def load_unit(u):
                b, half = divmod(u, 2)
                sp.wait_ge(scratch_done[b % 2], N_PARTS * (b // 2 + 1))
                if u >= RING:
                    sp.wait_ge(s2_done, TH * UB * (u - RING + 1))
                for hh in range(2):
                    rows = slice(QK_ROWS * hh, QK_ROWS * (hh + 1))
                    for dst, scratch in ((qp[u % RING][rows, hh], q_scratch), (kp[u % RING][rows], k_scratch)):
                        sp.dma_start(dst, scratch[b, :, 2 * half + hh].rearrange("s d j t -> s d (j t)")
                                     ).then_inc(packed[u % RING], 16)

            def load_max(u):
                sp.wait_ge(mT_kept, u + 1)
                for hh in range(2):
                    at, n = 2 * QK_ROWS + M_ROWS * hh, M_ROWS * UB
                    sp.dma_start(qp[u % RING][at:at + M_ROWS, hh], mT_sb[u % 2][n * hh:n * (hh + 1), :]
                                 ).then_inc(m_packed[u % RING], 16)

            write_parts(0)
            sp.wait_ge(preset, 1)
            sp.wait_ge(ones_set, 1)
            load_unit(0)
            load_unit(1)
            write_parts(1)
            load_unit(2)
            load_max(0)
            wb = [(gate_sb[:, :], gate), (up_sb[:, 0:RBLK], up), (up_sb[:, RBLK:FBLK], shup),
                  (down_sb[:, 0:RBLK], down), (down_sb[:, RBLK:FBLK], shdown), (sel_sb[:, :, :], sel)]
            wb += [(ebias_sb[:, c], ebias.unsqueeze(0).to_broadcast((P, E))) for c in range(C4)]
            assert len(wb) == N_WB

            for b in range(NB):
                if 2 * b + 3 < NU:
                    load_unit(2 * b + 3)
                load_max(2 * b + 1)
                if b + 2 < NB:
                    write_parts(b + 2)
                    load_unit(2 * b + 4)
                if b + 1 < NB:
                    load_max(2 * b + 2)
                if b == 1:
                    for dst, src in wb:
                        sp.dma_start(dst, src).then_inc(wb_loaded, 16)

            od = out.rearrange("(n p) d -> p n d", p=P)
            for i in range(NTILE):
                sp.wait_ge(ot_done, i + 1)
                sp.dma_start(od[:, C4 * i:C4 * (i + 1)], ot[i % 2][:, :, :]).then_inc(stored[i % 2], 16)
            for par in range(2):
                sp.wait_ge(stored[par], 16 * (NTILE // 2))

        @block.gpsimd
        def _(pool):
            nc.gpsimd.memset(tiny[:, 0:1], 0.0).then_inc(tiny_set, 1)
            for i in range(RING):
                ins = nc.gpsimd.memset(qp[i][:, :, :, :].rearrange("p a b c -> p (a b c)").bitcast(F32), 0.0)
            ins.then_inc(preset, 1)
            nc.gpsimd.memset(m_zero[:, :, :, :], 0.0)
            for i in range(3):
                nc.gpsimd.memset(tied[i][:, :, :], 0.0)
            for i in range(2):
                nc.gpsimd.memset(vv[i][:, :, :, DK + 1:VC], 0.0)
                ins = nc.gpsimd.memset(vv[i][:, :, :, DK:DK + 1], 1.0)
            ins.then_inc(preset, 1)

            def split_max(u):
                pool.wait_ge(max_done, 2 * UB * (u + 1))
                if u >= 1:
                    pool.wait_ge(mT_done, u)
                link = Link(pool, mparts_link, 3 * u)
                m, zero = mneg[u % 2], m_zero[:, :, :, :]
                link(nc.gpsimd.tensor_tensor(m_parts[:, :, :, 0], m[:, :, :, :], zero, ALU.add))
                link(nc.gpsimd.tensor_tensor(m_rest[:, :, :, :], m[:, :, :, :], m_parts[:, :, :, 0], ALU.subtract))
                link(nc.gpsimd.tensor_tensor(m_parts[:, :, :, 1], m_rest[:, :, :, :], zero, ALU.add))
                nc.gpsimd.tensor_tensor(m_parts[:, :, :, 2], m_rest[:, :, :, :], m_parts[:, :, :, 1],
                                        ALU.subtract).then_inc(mparts_done, 1)

            def norm(i, link_sem, stats_sem, st, work, rs, nm, used, ready):
                link = Link(pool, link_sem, LN_LINKS * i)
                pool.wait_ge(stats_sem, i + 1)
                norm_chain(nc.gpsimd, pool.wait_ge, link, st[:, :, :],
                           [w[:, :] for w in work], rs[:, :], nm[:, :],
                           (used, i) if i >= 1 else None).then_inc(ready, 1)
                assert link.n == LN_LINKS

            def chain_y(i):
                norm(i, ln2_link, y_stats, stats2, work2, rs2, nm2, yn_done, ln2_done)

            def chain_x1(i):
                norm(i, ln3_link, x1_stats, stats3, work3, rs3, nm3, xn2_done, ln3_done)

            def chain_f(i):
                norm(i, ln4_link, f_stats, stats4, work4, rs4, nm4, fn_done, ln4_done)

            def residual1(i):
                pool.wait_ge(yn_done, i + 1)
                xi = xbig[:, C4 * i:C4 * (i + 1)]
                nc.gpsimd.tensor_tensor(xi, xi, yn[:, :, :], ALU.add).then_inc(x1_done, 1)

            def residual2(i):
                pool.wait_ge(fn_done, i + 1)
                if i >= 2:
                    pool.wait_ge(stored[i % 2], 16 * (i // 2))
                nc.gpsimd.tensor_tensor(ot[i % 2][:, :, :], xbig[:, C4 * i:C4 * (i + 1)], fn[:, :, :],
                                        ALU.add).then_inc(ot_done, 1)

            for u in range(NU):
                split_max(u)
                if u == 2:
                    pool.wait_ge(ln1_stats, 1)
                    norm_chain(nc.gpsimd, pool.wait_ge, Link(pool, ln1_rest_link, 0), stats[:, SECOND:NT],
                               [w[:, SECOND:NT] for w in (nw_v, nw_t, nw_m, nw_d, nw_h)],
                               rs1[:, SECOND:NT], nm1[:, SECOND:NT]).then_inc(ln1_rest_done, 1)
                for i in range(2):
                    if u == 2 * PREP[i] + 2:
                        chain_y(i)
                    if u == 2 * PREP[i] + 3:
                        residual1(i)
                        chain_x1(i)
            for i in range(NTILE):
                if i + 2 < NTILE:
                    chain_y(i + 2)
                    residual1(i + 2)
                if i >= 1:
                    chain_f(i - 1)
                if i + 2 < NTILE:
                    chain_x1(i + 2)
                if i >= 1:
                    residual2(i - 1)
            chain_f(NTILE - 1)
            residual2(NTILE - 1)

        @block.scalar
        def _(act):
            def normalise(out_, in_, rs, nm):
                return nc.scalar.activation(out_, in_, ACT.Identity, bias=nm, scale=rs)

            def copy(out_, in_):
                return nc.scalar.activation(out_, in_, ACT.Copy)

            def norm_x(b):
                act.wait_ge(ln1_done, 1 if TH * b < FIRST else 2)
                if TH * b >= SECOND:
                    act.wait_ge(ln1_rest_done, 1)
                if b >= 1:
                    act.wait_ge(xnT_done, b)
                for th in range(TH):
                    t = TH * b + th
                    ins = normalise(xn[:, th], xbig[:, t], rs1[:, t:t + 1], nm1[:, t:t + 1])
                ins.then_inc(xn_done, 1)

            def keep_xnT(b):
                act.wait_ge(xnT_done, b + 1)
                if b >= 2:
                    act.wait_ge(v_done, b - 1)
                copy(xnT[b % 2][:, :], pX[:, 0:T]).then_inc(xnT_kept, 1)

            def part1(b):
                act.wait_ge(qk_done, b + 1)
                if b >= 2:
                    act.wait_ge(scratch_done[b % 2], N_PARTS * (b // 2))
                nc.scalar.activation(q_parts[b % 2][:, 0], pX[:, 0:T], ACT.Identity, bias=bqk_sb[:, 0:1])
                nc.scalar.activation(k_parts[b % 2][:, 0], pX[:, T:2 * T], ACT.Identity,
                                     bias=bqk_sb[:, 1:2]).then_inc(part1_done, 1)

            def part2(b):
                act.wait_ge(rest_done, b + 1)
                copy(q_parts[b % 2][:, 1], q_rest[:, :])
                copy(k_parts[b % 2][:, 1], k_rest[:, :]).then_inc(part2_done, 1)

            def keep_mT(u):
                act.wait_ge(mT_done, u + 1)
                if u >= 2:
                    act.wait_ge(m_packed[(u - 2) % RING], 2 * 16 * ((u - 2) // RING + 1))
                copy(mT_sb[u % 2][:, :], pXb[0:2 * M_ROWS * UB, 0:T]).then_inc(mT_kept, 1)

            def exp(b, j):
                if b >= 1:
                    act.wait_ge(pv_done, 4 * (b - 1) + j // 2 + 1)
                for sh in range(TH):
                    n = TH * (NBLK * b + j) + sh
                    act.wait_ge(s2_done, n + 1)
                    nc.scalar.activation(probs[j][:, sh], pS2[n % S2_RING][:, :, :], ACT.Exp,
                                         scale=SCALE).then_inc(exp_done, 1)

            def keep_oT(b, half):
                act.wait_ge(pv_done, 4 * b + 2 * half + 2)
                if b >= 1:
                    act.wait_ge(o_done, TH * b)
                copy(oT_sb[:, 2 * half:2 * half + 2, :], pO[:, :, :]).then_inc(oT_kept, 1)

            def keep_onT(b):
                act.wait_ge(onT_done, b + 1)
                if b >= 1:
                    act.wait_ge(y_done, b)
                copy(onT[:, :], pY[:, 0:T]).then_inc(onT_kept, 1)

            def norm_y(i, c):
                if c == 0:
                    act.wait_ge(ln2_done, i + 1)
                    if i >= 1:
                        act.wait_ge(x1_done, i)
                for cc in (c, c + 1):
                    ins = normalise(yn[:, cc], ybig[:, C4 * i + cc], rs2[:, cc:cc + 1], nm2[:, cc:cc + 1])
                if c:
                    ins.then_inc(yn_done, 1)

            def norm_x1(i, c):
                if c == 0:
                    act.wait_ge(ln3_done, i + 1)
                    if i >= 1:
                        act.wait_ge(x2T_done, i)
                for cc in (c, c + 1):
                    ins = normalise(xn2[:, cc], xbig[:, C4 * i + cc], rs3[:, cc:cc + 1], nm3[:, cc:cc + 1])
                if c:
                    ins.then_inc(xn2_done, 1)

            def keep_xT(i):
                act.wait_ge(x2T_done, i + 1)
                if i >= 2:
                    act.wait_ge(up_done, FBLK * (i - 1))
                copy(xT[i % 2][:, :], pX[:, :]).then_inc(xT_kept, 1)

            def exp_logits(i):
                act.wait_ge(logit_done, i + 1)
                if i >= 1:
                    act.wait_ge(cparts_done, i)
                nc.scalar.activation(e_sb[:, :, :], pX[:, 0:C4 * E], ACT.Exp, scale=-1.0).then_inc(e_done, 1)

            def keep_cT(i):
                act.wait_ge(cT_done, i + 1)
                if i >= 2:
                    act.wait_ge(spread_done, RBLK * (i - 1))
                copy(cT[i % 2][:, :], pXb[0:3 * E, 0:TILE]).then_inc(cT_kept, 1)

            def relu_square(i, k):
                n = FBLK * i + k
                act.wait_ge(up_done, n + 1)
                nc.scalar.activation(r_sb[k % 2][:, :], pU[k % 2], ACT.Relu).then_inc(relu_done, 1)
                act.wait_ge(relu_done, n + 1)
                if k < RBLK:
                    if RBLK * i + k >= 2:
                        act.wait_ge(h_done, RBLK * i + k - 1)
                    dst = r2_sb[k % 2]
                else:
                    act.wait_ge(down_done, n - HRING + 1)
                    dst = h_sb[n % HRING]
                nc.scalar.activation(dst[:, :], r_sb[k % 2][:, :], ACT.Square).then_inc(sq_done, 1)

            def keep_fT(i):
                act.wait_ge(down_done, FBLK * (i + 1))
                if i >= 1:
                    act.wait_ge(f_done, i)
                copy(fT_sb[:, :], pF[i % 2]).then_inc(fT_kept, 1)

            def norm_f(i, c):
                if c == 0:
                    act.wait_ge(ln4_done, i + 1)
                    if i >= 1:
                        act.wait_ge(ot_done, i)
                for cc in (c, c + 1):
                    ins = normalise(fn[:, cc], pN[:, D * cc:D * (cc + 1)], rs4[:, cc:cc + 1], nm4[:, cc:cc + 1])
                if c:
                    ins.then_inc(fn_done, 1)

            act.wait_ge(tiny_set, 1)
            nc.scalar.activation(tiny[:, 1:2], tiny[:, 0:1], ACT.Exp)
            act.wait_ge(wqk_loaded, 16 * N_WQK)
            act.wait_ge(xq_loaded[0], 16)
            for b in range(AHEAD):
                norm_x(b)
                keep_xnT(b)
                part1(b)
                if b + 1 < AHEAD:
                    part2(b)
            keep_mT(0)
            act.wait_ge(xq_loaded[1], 16)

            for b in range(NB):
                proj = b + AHEAD < NB
                for j in range(NBLK):
                    exp(b, j)
                    if j == 0:
                        if b - 1 + AHEAD < NB:
                            part2(b - 1 + AHEAD)
                        keep_mT(2 * b + 1)
                    if j == 1 and b >= 1:
                        keep_oT(b - 1, 1)
                    if j == 2 and proj:
                        norm_x(b + AHEAD)
                    if j == 4:
                        if proj:
                            keep_xnT(b + AHEAD)
                        if b == NB - 2:
                            keep_xT(0)
                        if b >= 1:
                            keep_onT(b - 1)
                    if j == 5:
                        if b + 1 < NB:
                            keep_mT(2 * b + 2)
                        keep_oT(b, 0)
                    if j == 6 and proj:
                        part1(b + AHEAD)
                    if j == 7:
                        if b == NB - 2:
                            exp_logits(0)
                    if b in PREP and j in (6, 7):
                        norm_y(PREP.index(b), 2 * (j - 6))
                    if b == PREP[0] + 2 and j in (2, 3):
                        norm_x1(0, 2 * (j - 2))
                    if b == NB - 1 and j in (2, 3):
                        norm_x1(1, 2 * (j - 2))

            for i in range(NTILE):
                for k in range(FBLK):
                    relu_square(i, k)
                    if i == 0 and k == 1:
                        keep_cT(0)
                    if i == 0:
                        if k == 0:
                            keep_oT(NB - 1, 1)
                        if k == 7:
                            keep_onT(NB - 1)
                    if i + 1 < NTILE:
                        if k == 1:
                            keep_xT(i + 1)
                        if k == 2:
                            exp_logits(i + 1)
                        if k == 16:
                            keep_cT(i + 1)
                    if i + 2 < NTILE:
                        if k in (4, 5):
                            norm_y(i + 2, 2 * (k - 4))
                        if k in (12, 13):
                            norm_x1(i + 2, 2 * (k - 12))
                    if i >= 1:
                        if k == 3:
                            keep_fT(i - 1)
                        if k in (9, 10):
                            norm_f(i - 1, 2 * (k - 9))
            keep_fT(NTILE - 1)
            norm_f(NTILE - 1, 0)
            norm_f(NTILE - 1, 2)

        @block.vector
        def _(dve):
            def rest(b):
                dve.wait_ge(part1_done, b + 1)
                if b >= 1:
                    dve.wait_ge(part3_done, b)
                for i, (left, parts) in enumerate(((q_rest, q_parts[b % 2]), (k_rest, k_parts[b % 2]))):
                    ins = nc.vector.scalar_tensor_tensor(out=left[:, :], in0=pX[:, T * i:T * (i + 1)],
                                                         scalar=bqk_sb[:, i:i + 1], in1=parts[:, 0],
                                                         op0=ALU.add, op1=ALU.subtract)
                ins.then_inc(rest_done, 1)

            def part3(b):
                dve.wait_ge(part2_done, b + 1)
                nc.vector.tensor_tensor(q_parts[b % 2][:, 2], q_rest[:, :], q_parts[b % 2][:, 1], ALU.subtract)
                nc.vector.tensor_tensor(k_parts[b % 2][:, 2], k_rest[:, :], k_parts[b % 2][:, 1], ALU.subtract).then_inc(part3_done, 1)

            def keep_v(b):
                dve.wait_ge(v_done, b + 1)
                if b >= 2:
                    dve.wait_ge(pv_done, 4 * (b - 1))
                nc.vector.tensor_tensor(vv[b % 2][:, :, :, 0:DK],
                                        pY[:, 0:T].rearrange("p (a h d) -> p a h d", a=TH, h=H),
                                        bv_sb[:, :, :].rearrange("p a (h d) -> p a h d", h=H),
                                        ALU.add).then_inc(v_kept, 1)

            def row_max(u, k):
                if k == 0 and u >= 2:
                    dve.wait_ge(mparts_done, u - 1)
                for hh in range(2):
                    dve.wait_ge(s1_done, 2 * (UB * u + k) + hh + 1)
                    nc.vector.tensor_reduce(mneg[u % 2][:, :, hh, k], pS1[hh][:, :].rearrange("p (a s) -> p a s", a=TH),
                                            AX.X, ALU.max, negate=True).then_inc(max_done, 1)

            def norm_o(b, th):
                dve.wait_ge(o_done, TH * b + th + 1)
                o = (pX, pY)[th][:, :].rearrange("p (h c) -> p h c", c=VC)
                nc.vector.reciprocal(o_rec[:, th], o[:, :, DK]).then_inc(rec_done, 1)
                dve.wait_ge(rec_done, TH * b + th + 1)
                if b >= 1:
                    dve.wait_ge(onT_done, b)
                nc.vector.tensor_tensor(o_sb[:, th].rearrange("p (h d) -> p h d", h=H), o[:, :, 0:DK],
                                        o_rec[:, th].unsqueeze(2).to_broadcast((P, H, DK)),
                                        ALU.mult).then_inc(o_kept, 1)

            def keep_y(b):
                dve.wait_ge(y_done, b + 1)
                nc.vector.tensor_tensor(ybig[:, TH * b:TH * (b + 1)],
                                        pY[:, 0:T].rearrange("p (a e) -> p a e", a=TH), bo_sb[:, :, :],
                                        ALU.add).then_inc(y_kept, 1)

            def stats_y(i):
                dve.wait_ge(y_kept, 2 * (i + 1))
                if i >= 1:
                    dve.wait_ge(ln2_done, i)
                for c in range(C4):
                    ins = nc.vector.bn_stats(stats2[:, c, :], ybig[:, C4 * i + c])
                ins.then_inc(y_stats, 1)

            def stats_x1(i):
                dve.wait_ge(x1_done, i + 1)
                if i >= 1:
                    dve.wait_ge(ln3_done, i)
                for c in range(C4):
                    ins = nc.vector.bn_stats(stats3[:, c, :], xbig[:, C4 * i + c])
                ins.then_inc(x1_stats, 1)

            def stats_f(i):
                dve.wait_ge(f_done, i + 1)
                if i >= 1:
                    dve.wait_ge(ln4_done, i)
                for c in range(C4):
                    ins = nc.vector.bn_stats(stats4[:, c, :], pN[:, D * c:D * (c + 1)])
                ins.then_inc(f_stats, 1)

            def norm1(link, t0, t1):
                n = t1 - t0
                for t in range(t0, t1):
                    ins = nc.vector.bn_stats(stats[:, t, :], xbig[:, t])
                link(ins)
                norm_chain(nc.vector, dve.wait_ge, link, stats[:, t0:t1],
                           [w[:, 0:n] for w in (nw_v, nw_t, nw_m, nw_d, nw_h)],
                           rs1[:, t0:t1], nm1[:, t0:t1]).then_inc(ln1_done, 1)

            PAD = E // 2
            flat = lambda i, n, s=0: tied[i][:, :, PAD - s:PAD - s + n]

            def pick_ties(link, values, n, at):
                least = top8[:, :, at - 1:at].to_broadcast((P, C4, n))
                nc.vector.tensor_tensor(above[:, :, 0:n], values, least, ALU.is_gt)
                link(nc.vector.tensor_tensor(flat(0, n), values, least, ALU.is_equal))

            def pick_need(link, n, want):
                link(nc.vector.tensor_reduce(need[:, :], above[:, :, 0:n], AX.X, ALU.add))
                link(nc.vector.tensor_scalar(need[:, :], need[:, :], -1.0, float(want), ALU.mult, ALU.add))

            def pick_prefix(link, n, steps):
                for s in steps:
                    src, dst = 0 if s == 0 else 2 - s % 2, 1 + s % 2
                    link(nc.vector.tensor_tensor(flat(dst, n), flat(src, n), flat(src, n, 1 << s), ALU.add))

            def pick_fill(link, n, steps, picked_):
                src = 2 - steps % 2
                link(nc.vector.tensor_tensor(picked_, flat(src, n), need[:, :].unsqueeze(2).to_broadcast((P, C4, n)),
                                             ALU.is_le))
                link(nc.vector.tensor_tensor(picked_, picked_, flat(0, n), ALU.mult))
                link(nc.vector.tensor_tensor(picked_, picked_, above[:, :, 0:n], ALU.add))

            def route(link, i, step):
                g = choice[:, :, :].rearrange("p c (g m) -> p (c g) m", g=GROUPS)
                if step == 0:
                    dve.wait_ge(e_done, i + 1)
                    link(nc.vector.tensor_scalar(score[:, :, :], e_sb[:, :, :], 1.0, None, ALU.add))
                    link(nc.vector.reciprocal(score[:, :, :], score[:, :, :]))
                if step == 1:
                    link(nc.vector.tensor_tensor(choice[:, :, :], score[:, :, :], ebias_sb[:, :, :], ALU.add))
                    nc.vector.tensor_tensor(pair_hi[:, :, :], g[:, :, 0:2], g[:, :, 2:4], ALU.max)
                    link(nc.vector.tensor_tensor(pair_lo[:, :, :], g[:, :, 0:2], g[:, :, 2:4], ALU.min))
                    nc.vector.tensor_tensor(g_top[:, :], pair_hi[:, :, 0], pair_hi[:, :, 1], ALU.max)
                    nc.vector.tensor_tensor(g_mid[:, :], pair_hi[:, :, 0], pair_hi[:, :, 1], ALU.min)
                    link(nc.vector.tensor_tensor(g_low[:, :], pair_lo[:, :, 0], pair_lo[:, :, 1], ALU.max))
                if step == 2:
                    link(nc.vector.tensor_tensor(g_mid[:, :], g_mid[:, :], g_low[:, :], ALU.max))
                    link(nc.vector.tensor_tensor(g_score[:, :, :].rearrange("p c g -> p (c g)"), g_top[:, :],
                                                 g_mid[:, :], ALU.add))
                    for c in range(C4):
                        ins = nc.vector.max(top8[:, c], g_score[:, c])
                    link(ins)
                if step == 3:
                    pick_ties(link, g_score[:, :, :], GROUPS, TOPG)
                    pick_need(link, GROUPS, TOPG)
                    pick_prefix(link, GROUPS, (0,))
                if step == 4:
                    pick_prefix(link, GROUPS, (1, 2))
                    pick_fill(link, GROUPS, 3, picked_g[:, :, :])
                if step == 5:
                    link(nc.vector.tensor_tensor(g, g, picked_g[:, :, :].rearrange("p c g -> p (c g)").unsqueeze(2)
                                                 .to_broadcast((P, C4 * GROUPS, E // GROUPS)), ALU.mult))
                    for c in range(C4):
                        ins = nc.vector.max(top8[:, c], choice[:, c])
                    link(ins)
                if step == 6:
                    pick_ties(link, choice[:, :, :], E, TOPK)
                    pick_need(link, E, TOPK)
                if step == 7:
                    pick_prefix(link, E, (0, 1, 2))
                if step == 8:
                    pick_prefix(link, E, (3, 4))
                if step == 9:
                    pick_fill(link, E, 5, picked[:, :, :])
                if step == 10:
                    link(nc.vector.tensor_tensor(comb[:, :, :], score[:, :, :], picked[:, :, :], ALU.mult))
                    link(nc.vector.tensor_reduce(w_sum[:, :], comb[:, :, :], AX.X, ALU.add))
                    link(nc.vector.tensor_scalar(w_sum[:, :], w_sum[:, :], 1e-20, None, ALU.add))
                    link(nc.vector.reciprocal(w_sum[:, :], w_sum[:, :]))
                if step == 11:
                    link(nc.vector.scalar_tensor_tensor(out=comb[:, :, :], in0=comb[:, :, :], scalar=ROUTED_SCALE,
                                                        in1=w_sum[:, :].unsqueeze(2).to_broadcast((P, C4, E)),
                                                        op0=ALU.mult, op1=ALU.mult))
                    if i >= 1:
                        dve.wait_ge(cT_done, i)
                    link(nc.vector.tensor_copy(c_parts[:, :, 0], comb[:, :, :]))
                    link(nc.vector.tensor_tensor(c_rest[:, :, :], comb[:, :, :], c_parts[:, :, 0], ALU.subtract))
                    link(nc.vector.tensor_copy(c_parts[:, :, 1], c_rest[:, :, :]))
                    nc.vector.tensor_tensor(c_parts[:, :, 2], c_rest[:, :, :], c_parts[:, :, 1],
                                            ALU.subtract).then_inc(cparts_done, 1)
                    assert link.n == RT_LINKS, link.n

            def weigh(i, k):
                n = FBLK * i + k
                dve.wait_ge(sq_done, n + 1)
                dve.wait_ge(spread_done, RBLK * i + k + 1)
                if n >= HRING:
                    dve.wait_ge(down_done, n - HRING + 1)
                nc.vector.tensor_tensor(h_sb[n % HRING][:, :], pC[k % 2], r2_sb[k % 2][:, :],
                                        ALU.mult).then_inc(h_done, 1)

            link = Link(dve, ln1_link, 0)
            dve.wait_ge(xq_loaded[0], 16)
            norm1(link, 0, FIRST)
            for i in range(RING):
                ins = nc.vector.memset(kp[i][2 * QK_ROWS:P, :, :], 1.0)
            ins.then_inc(ones_set, 1)
            dve.wait_ge(wqk_loaded, 16 * N_WQK)
            rest(0)
            part3(0)
            dve.wait_ge(wa_loaded, 16 * N_WA)
            dve.wait_ge(preset, 2)
            keep_v(0)
            rest(1)
            part3(1)
            rest(2)
            dve.wait_ge(xq_loaded[1], 16)
            norm1(link, FIRST, SECOND)
            for u in range(2):
                for k in range(UB):
                    row_max(u, k)

            rt = Link(dve, rt_link, 0)
            for b in range(NB):
                last = b == NB - 1
                for j in range(NBLK):
                    if b == 0 and j < 5:
                        n = (NT - SECOND) // 5
                        for t in range(SECOND + n * j, SECOND + n * (j + 1)):
                            ins = nc.vector.bn_stats(stats[:, t, :], xbig[:, t])
                        if j == 4:
                            ins.then_inc(ln1_stats, 1)
                    if b + 1 < NB:
                        row_max(2 * b + 2 + j // UB, j % UB)
                    if j == 1:
                        if b - 1 + AHEAD < NB:
                            part3(b - 1 + AHEAD)
                        if b + 1 < NB:
                            keep_v(b + 1)
                    if j in (2, 3) and b >= 1:
                        norm_o(b - 1, j - 2)
                    if j == 6 and b >= 1:
                        keep_y(b - 1)
                    if j == 7 and b + AHEAD < NB:
                        rest(b + AHEAD)
                    if b in PREP and j == 2:
                        stats_y(PREP.index(b))
                    if b - 1 in PREP and j == 0:
                        stats_x1(PREP.index(b - 1))
                    if last and j < 6:
                        if j == 0:
                            dve.wait_ge(wb_loaded, 16 * N_WB)
                        route(rt, 0, 2 * j)
                        route(rt, 0, 2 * j + 1)

            for i in range(NTILE):
                rt = Link(dve, rt_link, RT_LINKS * (i + 1))
                for k in range(RBLK):
                    weigh(i, k)
                    if i == 0:
                        if k in (4, 5):
                            norm_o(NB - 1, k - 4)
                        if k == 10:
                            keep_y(NB - 1)
                    if i + 1 < NTILE and 3 <= k < 15:
                        route(rt, i + 1, k - 3)
                    if i + 2 < NTILE:
                        if k == 0:
                            stats_y(i + 2)
                        if k == 8:
                            stats_x1(i + 2)
                    if i >= 1 and k == 5:
                        stats_f(i - 1)
            stats_f(NTILE - 1)

        @block.tensor
        def _(pe):
            mm, tr = nc.tensor.matmul, nc.tensor.transpose

            def transpose_x(b):
                pe.wait_ge(xn_done, b + 1)
                for th in range(TH):
                    ins = tr(pX[:, P * th:P * (th + 1)], xn[:, th], idf[:, :])
                ins.then_inc(xnT_done, 1)

            def project_qk(b):
                pe.wait_ge(xnT_kept, b + 1)
                mm(pX[:, 0:T], wq_sb[:, :], xnT[b % 2][:, :], start=True, stop=True)
                mm(pX[:, T:2 * T], wk_sb[:, :], xnT[b % 2][:, :], start=True, stop=True).then_inc(qk_done, 1)

            def project_v(b):
                pe.wait_ge(xnT_kept, b + 1)
                for th in range(TH):
                    ins = mm(pY[:, D * th:D * (th + 1)], xnT[b % 2][:, P * th:P * (th + 1)], wv_sb[:, :],
                             start=True, stop=True)
                ins.then_inc(v_done, 1)

            def scores_by_query(u, k, hh):
                slot, n = u % RING, 2 * (UB * u + k) + hh
                if k == 0 and hh == 0:
                    pe.wait_ge(packed[slot], 4 * 16 * (u // RING + 1))
                if n >= 2:
                    pe.wait_ge(max_done, n - 1)
                for th in range(TH):
                    ins = mm(pS1[hh][:, T * th:T * (th + 1)], qp[slot][0:2 * QK_ROWS, hh, k, P * th:P * (th + 1)],
                             kp[slot][0:2 * QK_ROWS, k, :], start=True, stop=True)
                ins.then_inc(s1_done, 1)

            def scores_by_key(b, j, sh):
                u, k = 2 * b + j // UB, j % UB
                slot, n = u % RING, TH * (NBLK * b + j) + sh
                if k == 0 and sh == 0:
                    pe.wait_ge(m_packed[slot], 2 * 16 * (u // RING + 1))
                if n >= S2_RING:
                    pe.wait_ge(exp_done, n - S2_RING + 1)
                mm(pS2[n % S2_RING][:, :, :], kp[slot][0:DIFF_ROWS, k, P * sh:P * (sh + 1)],
                   qp[slot][0:DIFF_ROWS, :, k, :], start=True, stop=True).then_inc(s2_done, 1)

            def outputs(b, g):
                pe.wait_ge(exp_done, TH * (NBLK * b + 2 * g + 2))
                if g == 0:
                    pe.wait_ge(v_kept, b + 1)
                if g % 2 == 0 and 2 * b + g // 2 >= 1:
                    pe.wait_ge(oT_kept, 2 * b + g // 2)
                for sh in range(TH):
                    for h in range(4):
                        ins = mm(pO[VC * h:VC * (h + 1), g % 2], vv[b % 2][:, sh, 4 * g + h, :],
                                 probs[2 * g + h // 2][:, sh, h % 2, :], start=sh == 0, stop=sh == TH - 1)
                ins.then_inc(pv_done, 1)

            def transpose_max(u):
                pe.wait_ge(mparts_done, u + 1)
                for th in range(TH):
                    ins = tr(pXb[0:2 * M_ROWS * UB, P * th:P * (th + 1)],
                             m_parts[:, th].rearrange("p a b c -> p (a b c)"), idb[:, :])
                ins.then_inc(mT_done, 1)

            def transpose_o(b, th):
                pe.wait_ge(oT_kept, 2 * b + 2)
                for g in range(4):
                    ins = tr((pX, pY)[th][:, P * g:P * (g + 1)], oT_sb[:, g, P * th:P * (th + 1)], idf[:, :])
                ins.then_inc(o_done, 1)

            def transpose_on(b):
                pe.wait_ge(o_kept, TH * (b + 1))
                for th in range(TH):
                    ins = tr(pY[:, P * th:P * (th + 1)], o_sb[:, th], idf[:, :])
                ins.then_inc(onT_done, 1)

            def project_y(b):
                pe.wait_ge(onT_kept, b + 1)
                for th in range(TH):
                    ins = mm(pY[:, D * th:D * (th + 1)], onT[:, P * th:P * (th + 1)], wo_sb[:, :],
                             start=True, stop=True)
                ins.then_inc(y_done, 1)

            def transpose_x1(i):
                pe.wait_ge(xn2_done, i + 1)
                for c in range(C4):
                    ins = tr(pX[:, P * c:P * (c + 1)], xn2[:, c], idf[:, :])
                ins.then_inc(x2T_done, 1)

            def logits(i):
                pe.wait_ge(xT_kept, i + 1)
                for c in range(C4):
                    ins = mm(pX[:, E * c:E * (c + 1)], xT[i % 2][:, P * c:P * (c + 1)], gate_sb[:, :],
                             start=True, stop=True)
                ins.then_inc(logit_done, 1)

            def transpose_c(i):
                pe.wait_ge(cparts_done, i + 1)
                for c in range(C4):
                    ins = tr(pXb[0:3 * E, P * c:P * (c + 1)], c_parts[:, c].rearrange("p a e -> p (a e)"), idb[:, :])
                ins.then_inc(cT_done, 1)

            def up_block(i, k):
                n = FBLK * i + k
                if n >= 2:
                    pe.wait_ge(relu_done, n - 1)
                mm(pU[k % 2], up_sb[:, k], xT[i % 2][:, :], start=True, stop=True).then_inc(up_done, 1)

            def spread_block(i, k):
                if k == 0:
                    pe.wait_ge(cT_kept, i + 1)
                if RBLK * i + k >= 2:
                    pe.wait_ge(h_done, RBLK * i + k - 1)
                mm(pC[k % 2], sel_sb[:, k], cT[i % 2][:, :], start=True, stop=True).then_inc(spread_done, 1)

            def down_block(n):
                i, k = divmod(n, FBLK)
                if k < RBLK:
                    pe.wait_ge(h_done, RBLK * i + k + 1)
                else:
                    pe.wait_ge(sq_done, n + 1)
                if k == 0 and i >= 2:
                    pe.wait_ge(fT_kept, i - 1)
                if k == 0 and i == 1:
                    pe.wait_ge(y_kept, NB)
                mm(pF[i % 2], down_sb[:, k], h_sb[n % HRING][:, :], start=k == 0,
                   stop=k == FBLK - 1).then_inc(down_done, 1)

            def transpose_f(i):
                pe.wait_ge(fT_kept, i + 1)
                if i >= 1:
                    pe.wait_ge(fn_done, i)
                for c in range(C4):
                    ins = tr(pN[:, P * c:P * (c + 1)], fT_sb[:, P * c:P * (c + 1)], idf[:, :])
                ins.then_inc(f_done, 1)

            pe.wait_ge(wqk_loaded, 16 * N_WQK)
            for b in range(AHEAD):
                if b >= 1:
                    pe.wait_ge(rest_done, b)
                transpose_x(b)
                project_qk(b)
                if b == 0:
                    pe.wait_ge(wa_loaded, 16 * N_WA)
                    project_v(0)
            pe.wait_ge(rest_done, AHEAD)
            for u in range(2):
                for k in range(UB):
                    for hh in range(2):
                        scores_by_query(u, k, hh)
                if u == 0:
                    transpose_max(0)

            for b in range(NB):
                proj = b + AHEAD < NB
                last = b == NB - 1
                for j in range(NBLK):
                    for hh in range(2):
                        if not last:
                            scores_by_query(2 * b + 2 + j // UB, j % UB, hh)
                        scores_by_key(b, j, hh)
                        if j == 6 and hh == 0 and proj:
                            pe.wait_ge(mT_kept, 2 * b + 3)
                            project_qk(b + AHEAD)
                    if j == 0:
                        if b - 1 + AHEAD < NB:
                            pe.wait_ge(rest_done, b + AHEAD)
                        elif last:
                            pe.wait_ge(e_done, 1)
                        transpose_max(2 * b + 1)
                    if j == 1:
                        if b >= 1:
                            outputs(b - 1, 3)
                        if not last:
                            if b >= 2:
                                pe.wait_ge(y_kept, b - 1)
                            project_v(b + 1)
                    if j == 2 and b >= 1:
                        pe.wait_ge(mT_kept, 2 * b + 2)
                        transpose_o(b - 1, 0)
                    if j == 3:
                        if b >= 1:
                            pe.wait_ge(*((y_kept, b - 1) if last else (v_kept, b + 2)))
                            transpose_o(b - 1, 1)
                        outputs(b, 0)
                    if j == 4:
                        pe.wait_ge(*((o_kept, TH * (b - 1) + 1) if b >= 1 else (mT_kept, 2)))
                        if proj:
                            transpose_x(b + AHEAD)
                        if b == NB - 2:
                            transpose_x1(0)
                        if b >= 1:
                            transpose_on(b - 1)
                    if j == 5:
                        if not last:
                            if proj:
                                pe.wait_ge(xnT_kept, b + AHEAD + 1)
                            elif b == NB - 2:
                                pe.wait_ge(xT_kept, 1)
                            transpose_max(2 * b + 2)
                        if b >= 1:
                            project_y(b - 1)
                        outputs(b, 1)
                    if j == 6 and b == NB - 2:
                        pe.wait_ge(mT_kept, 2 * b + 3)
                        pe.wait_ge(wb_loaded, 16 * N_WB)
                        logits(0)
                    if j == 7:
                        outputs(b, 2)

            pe.wait_ge(max_done, H * NB)
            pe.wait_ge(exp_done, TH * NBLK * NB)
            for i in range(NTILE):
                for k in range(FBLK):
                    n = FBLK * i + k
                    up_block(i, k)
                    if n >= LAG:
                        down_block(n - LAG)
                    if i == 0 and k == 0:
                        outputs(NB - 1, 3)
                    elif i == 0 and k == 1:
                        transpose_c(0)
                        spread_block(0, 0)
                        spread_block(0, 1)
                    elif k < RBLK:
                        spread_block(i, k)
                    if i == 0:
                        if k == 4:
                            pe.wait_ge(e_done, 2)
                            transpose_o(NB - 1, 0)
                        if k == 5:
                            pe.wait_ge(y_kept, NB - 1)
                            transpose_o(NB - 1, 1)
                        if k == 7:
                            transpose_on(NB - 1)
                        if k == 9:
                            project_y(NB - 1)
                    elif k == 4:
                        pe.wait_ge(oT_kept, 2 * NB)
                        transpose_f(i - 1)
                    if i + 1 < NTILE:
                        if k == 1:
                            pe.wait_ge(cT_kept, i + 1)
                            transpose_x1(i + 1)
                        if k == 2:
                            logits(i + 1)
                        if k == 16:
                            transpose_c(i + 1)
            for n in range(FBLK * NTILE - LAG, FBLK * NTILE):
                down_block(n)
            transpose_f(NTILE - 1)


def kernel(**inputs):
    import ml_dtypes
    import concourse.bacc as bacc
    from concourse.bass_utils import run_bass_kernel_spmd

    a = {k: np.asarray(v) for k, v in inputs.items()}
    order = lambda w: w.reshape((2, UB, 2, DK) + w.shape[1:]).transpose(
        (0, 2, 3, 1) + tuple(range(4, 3 + w.ndim))).reshape(w.shape)
    names = ["x", "wq", "wk", "wv", "wo", "bq", "bk", "bv", "bo", "gate", "ebias", "up", "shup", "down", "shdown",
             "ident_f", "ident_b", "sel"]
    sel = np.zeros((3, E, RBLK, P), ml_dtypes.bfloat16)
    for e in range(E):
        blk, at = divmod(e * EI, P)
        sel[:, e, blk, at:at + EI] = 1
    arrays = {
        "x": a["L0_attn_x"].reshape(NB * T, D),
        "wq": order(a["L0_attn_w_q"]).T,
        "wk": order(a["L0_attn_w_k"]).T,
        "wv": a["L0_attn_w_v"].T,
        "wo": a["L0_attn_w_o"].T,
        "bq": order(a["L0_attn_b_q"]),
        "bk": order(a["L0_attn_b_k"]),
        "bv": a["L0_attn_b_v"],
        "bo": a["L0_attn_b_o"],
        "gate": a["L0_ffn_gate_w"].T,
        "ebias": a["L0_ffn_e_bias"],
        "up": a["L0_ffn_up_w"].reshape(RBLK, P, D).transpose(2, 0, 1),
        "shup": a["L0_ffn_shared_up_w"].reshape(SI // P, P, D).transpose(2, 0, 1),
        "down": a["L0_ffn_down_w"].reshape(RBLK, P // EI, D, EI).transpose(1, 3, 0, 2).reshape(P, RBLK, D),
        "shdown": a["L0_ffn_shared_down_w"].reshape(D, SI // P, P).transpose(2, 1, 0),
        "ident_f": np.eye(P, dtype=np.float32),
        "ident_b": np.eye(P, dtype=ml_dtypes.bfloat16),
        "sel": sel.reshape(3 * E, RBLK, P),
    }
    nc = bacc.Bacc("TRN2", target_bir_lowering=False, num_devices=1)
    args, maps = [], {}
    for name in names:
        v = np.ascontiguousarray(arrays[name])
        maps[f"in_{name}"] = v
        args.append(nc.dram_tensor(f"in_{name}", v.shape, mybir.dt.from_np(v.dtype), kind="ExternalInput").ap())
    args.append(nc.dram_tensor("out_x", (NB * T, D), F32, kind="ExternalOutput").ap())
    block_kernel(nc, *args)
    r = run_bass_kernel_spmd(nc, [maps], core_ids=[0])
    return r.results[0]["out_x"].reshape(NB, T, D)
```

```python
from contextlib import ExitStack

import numpy as np

import concourse.bass as bass
from concourse import mybir

F32 = mybir.dt.float32
BF16 = mybir.dt.bfloat16
F32R = mybir.dt.float32r
I32 = mybir.dt.int32
ALU = mybir.AluOpType
ACT = mybir.ActivationFunctionType
AX = mybir.AxisListType

P = 128
NB, T, D = 16, 256, 128
H, DK = 16, 8
TH = T // P
NT = NB * TH
NBLK = H // 2
UB = NBLK // 2
NU = 2 * NB
SLOTS = 6
Q_PARTS = (0, 0, 0, 1, 1, 2)
K_PARTS = (0, 1, 2, 0, 1, 0)
QK_ROWS = SLOTS * DK
M_ROWS = 3
DIFF_ROWS = 2 * QK_ROWS + 2 * M_ROWS
RING = 4
S1_RING, S2_RING = 3, 2
SCALE = float(DK) ** -0.5
VC = 32

E, EI, GROUPS, TOPG, TOPK = 32, 64, 8, 4, 6
ROUTED_SCALE = 2.5
SI = 256
TILE = 512
NTILE = NB * T // TILE
C4 = TILE // P
RBLK = E * EI // P
FBLK = RBLK + SI // P
HRING = 4
AHEAD = 3
FIRST = TH * AHEAD
ROUTE_AT = ((3, 4, 5, 6, 7, 8, 9, 10, 11, 12, 13, 14),
            (0, 1, 2, 3, 4, 5, 6, 8, 9, 11, 12, 13))
NORM_Y_AT = ((3, 4, 5, 6), (1, 3, 4, 5))
NORM_X1_AT = ((12, 13, 14, 15), (11, 12, 13, 14))
ROUTE_FIRST = (((), (), (), (0,), (), (), (1,), ()),
               ((), (2,), (), (), (3,), (), (), (4,)),
               ((5, 6), (7,), (), (8, 9), (10, 11), (), (), ()))
PREP = (5, 8)
LAG = 3
HIGH_MASK = -(1 << 12)
CUT = TILE // P
NCUT = -(-FBLK // CUT)
CUT_BATCH = 4
EPS = 1e-5
RSQRT_MAGIC = 0x5F3759DF
LN_LINKS = 17
RT_LINKS = 38


class Link:

    def __init__(self, eng, sem, base):
        self.eng, self.sem, self.base, self.n = eng, sem, base, 0

    def __call__(self, instruction):
        self.n += 1
        instruction.then_inc(self.sem, 1)
        self.eng.wait_ge(self.sem, self.base + self.n)


def block_kernel(nc, x, wq, wk, wv, wo, bq, bk, bv, bo, gate, ebias, up, shup, down, shdown,
                 ident_f, ident_b, sel, out):
    with ExitStack() as ctx:
        def sb(name, shape, dt=F32):
            return ctx.enter_context(nc.sbuf_tensor(name, shape, dt))

        def ps(name, shape):
            return ctx.enter_context(nc.psum_tensor(name, shape, F32))

        def sem(name):
            return ctx.enter_context(nc.semaphore(name))

        q_scratch = nc.dram_tensor("q_scratch", (NB, SLOTS, 4, DK, UB, T), BF16).ap()
        k_scratch = nc.dram_tensor("k_scratch", (NB, SLOTS, 4, DK, UB, T), BF16).ap()

        xbig = sb("xbig", [P, NT, D])
        ybig = sb("ybig", [P, NT, D])
        wq_sb, wk_sb = sb("wq_sb", [P, D]), sb("wk_sb", [P, D])
        wv_sb, wo_sb = sb("wv_sb", [P, D]), sb("wo_sb", [P, D])
        bqk_sb = sb("bqk_sb", [P, 2])
        bv_sb, bo_sb = sb("bv_sb", [P, D]), sb("bo_sb", [P, D])
        gate_sb = sb("gate_sb", [P, E])
        ebias_sb = sb("ebias_sb", [P, C4, E])
        up_hi, up_lo = sb("up_hi", [P, FBLK, P], F32R), sb("up_lo", [P, FBLK, P], F32R)
        down_sb = sb("down_sb", [P, FBLK, D])
        idf, idb = sb("idf", [P, P]), sb("idb", [P, P], BF16)
        sel_sb = sb("sel_sb", [3 * E, RBLK, P], BF16)
        stats, stats2, stats3, stats4 = (sb(n, [P, c, 6]) for n, c in (
            ("stats", NT), ("stats2", C4), ("stats3", C4), ("stats4", C4)))
        rs1, nm1 = sb("rs1", [P, NT]), sb("nm1", [P, NT])
        rs2, nm2 = sb("rs2", [P, C4]), sb("nm2", [P, C4])
        rs3, nm3 = sb("rs3", [P, C4]), sb("nm3", [P, C4])
        rs4, nm4 = sb("rs4", [P, C4]), sb("nm4", [P, C4])
        nw_v, nw_t, nw_m, nw_d, nw_h = (sb(f"nw_{n}", [P, NT]) for n in "vtmdh")
        work2, work3, work4 = ([sb(f"work{k}_{n}", [P, C4]) for n in "vtmdh"] for k in (2, 3, 4))
        tiny = sb("tiny", [P, 2])
        xn = sb("xn", [P, TH, D])
        xnT = [sb(f"xnT{i}", [P, T]) for i in range(2)]
        q_parts = [sb(f"q_parts{i}", [P, 3, T], BF16) for i in range(2)]
        k_parts = [sb(f"k_parts{i}", [P, 3, T], BF16) for i in range(2)]
        q_rest, k_rest = sb("q_rest", [P, T]), sb("k_rest", [P, T])
        qp = [sb(f"qp{i}", [P, 2, UB, T], BF16) for i in range(RING)]
        kp = [sb(f"kp{i}", [P, UB, T], BF16) for i in range(RING)]
        vv = [sb(f"vv{i}", [P, TH, H, VC]) for i in range(2)]
        mneg = [sb(f"mneg{i}", [P, TH, 2, UB]) for i in range(2)]
        m_rest, m_zero = sb("m_rest", [P, TH, 2, UB]), sb("m_zero", [P, TH, 2, UB])
        m_parts = sb("m_parts", [P, TH, 2, M_ROWS, UB], BF16)
        mT_sb = [sb(f"mT{i}", [2 * M_ROWS * UB, T], BF16) for i in range(2)]
        probs = [sb(f"probs{j}", [P, TH, 2, T]) for j in range(NBLK)]
        oT_sb = sb("oT_sb", [P, 4, T])
        o_rec = sb("o_rec", [P, TH, H])
        o_sb = sb("o_sb", [P, TH, D])
        onT = sb("onT", [P, T])
        yn = sb("yn", [P, C4, D])
        xn2 = sb("xn2", [P, C4, D])
        xT = sb("xT", [P, TILE])
        x_hi, x_lo = ([qp[i][:, part].rearrange("p a b -> p (a b)").bitcast(F32R) for i in range(2)]
                      for part in range(2))
        x_cut = kp[0][:, :, :].rearrange("p a b -> p (a b)").bitcast(F32)
        e_sb = sb("e_sb", [P, C4, E])
        score, choice = sb("score", [P, C4, E]), sb("choice", [P, C4, E])
        pair_hi, pair_lo = sb("pair_hi", [P, C4 * GROUPS, 2]), sb("pair_lo", [P, C4 * GROUPS, 2])
        g_top, g_mid, g_low = (sb(f"g_{n}", [P, C4 * GROUPS]) for n in ("top", "mid", "low"))
        g_score = sb("g_score", [P, C4, GROUPS])
        top8 = sb("top8", [P, C4, 8])
        above, need = sb("above", [P, C4, E]), sb("need", [P, C4])
        tied = [sb(f"tied{i}", [P, C4, E // 2 + E]) for i in range(3)]
        picked_g, picked = sb("picked_g", [P, C4, GROUPS]), sb("picked", [P, C4, E])
        w_sum, comb, c_rest = sb("w_sum", [P, C4]), sb("comb", [P, C4, E]), sb("c_rest", [P, C4, E])
        c_parts = sb("c_parts", [P, C4, 3, E], BF16)
        cT = [sb(f"cT{i}", [3 * E, TILE], BF16) for i in range(2)]
        r_sb = [sb(f"r{i}", [P, TILE]) for i in range(2)]
        r2_sb = [sb(f"rr{i}", [P, TILE]) for i in range(2)]
        h_ring = sb("h_ring", [P, HRING, TILE])
        h_sb = [h_ring[:, i] for i in range(HRING)]
        fT_sb = sb("fT_sb", [P, TILE])
        assert HRING * TILE == RBLK * P and TILE >= SI
        up_in = [h_ring[:, i] for i in range(NCUT - 1)] + [fT_sb[:, 0:SI]]
        w_cut = r_sb[0]
        fn = sb("fn", [P, C4, D])
        ot = [sb(f"ot{i}", [P, C4, D]) for i in range(2)]

        pS1 = [ps(f"pS1_{i}", [P, TILE]) for i in range(S1_RING)]
        pS2 = [ps(f"pS2_{i}", [P, 2, T]) for i in range(S2_RING)]
        pO = ps("pO", [P, 2, T])
        pX, pY = ps("pX", [P, TILE]), ps("pY", [P, TILE])
        pXb = pX[:, :].bitcast(BF16)
        pU = [pS1[i][:, :] for i in range(2)]
        pC = [pS2[i][:, :, :].rearrange("p a b -> p (a b)") for i in range(2)]
        pF = [pS1[2][:, :], pY[:, :]]
        pN = pO[:, :, :].rearrange("p a b -> p (a b)")

        xq_loaded = [sem(f"xq_loaded{i}") for i in range(3)]
        wqk_loaded = sem("wqk_loaded")
        wa_loaded = sem("wa_loaded")
        wb_loaded = sem("wb_loaded")
        tiny_set = sem("tiny_set")
        preset = sem("preset")
        ones_set = sem("ones_set")
        ln1_done = sem("ln1_done")
        ln1_stats = sem("ln1_stats")
        ln1_rest_done = sem("ln1_rest_done")
        ln1_rest_link = sem("ln1_rest_link")
        ln1_link = sem("ln1_link")
        xn_done = sem("xn_done")
        xnT_done = sem("xnT_done")
        xnT_kept = sem("xnT_kept")
        qk_done = sem("qk_done")
        part1_done = sem("part1_done")
        rest_done = sem("rest_done")
        part2_done = sem("part2_done")
        part3_done = sem("part3_done")
        scratch_done = [sem(f"scratch_done{i}") for i in range(2)]
        packed = [sem(f"packed{i}") for i in range(RING)]
        v_done = sem("v_done")
        v_kept = sem("v_kept")
        s1_done = sem("s1_done")
        max_done = sem("max_done")
        mparts_done = sem("mparts_done")
        mparts_link = sem("mparts_link")
        mT_done = sem("mT_done")
        mT_kept = sem("mT_kept")
        m_packed = [sem(f"m_packed{i}") for i in range(RING)]
        s2_done = sem("s2_done")
        exp_done = sem("exp_done")
        pv_done = sem("pv_done")
        oT_kept = sem("oT_kept")
        o_done = sem("o_done")
        rec_done = sem("rec_done")
        o_kept = sem("o_kept")
        onT_done = sem("onT_done")
        onT_kept = sem("onT_kept")
        y_done = sem("y_done")
        y_kept = sem("y_kept")
        wcut_done = sem("wcut_done")
        whi_done = sem("whi_done")
        wlo_done = sem("wlo_done")
        ln2_link, ln3_link, ln4_link, rt_link = (sem(n) for n in ("ln2_link", "ln3_link", "ln4_link", "rt_link"))
        y_stats, x1_stats, f_stats = (sem(n) for n in ("y_stats", "x1_stats", "f_stats"))
        ln2_done = sem("ln2_done")
        yn_done = sem("yn_done")
        x1_done = sem("x1_done")
        ln3_done = sem("ln3_done")
        xn2_done = sem("xn2_done")
        x2T_done = sem("x2T_done")
        xT_kept = sem("xT_kept")
        xcut_done = sem("xcut_done")
        xhi_done = sem("xhi_done")
        xlo_done = sem("xlo_done")
        logit_done = sem("logit_done")
        e_done = sem("e_done")
        cparts_done = sem("cparts_done")
        cT_done = sem("cT_done")
        cT_kept = sem("cT_kept")
        up_done = sem("up_done")
        relu_done = sem("relu_done")
        sq_done = sem("sq_done")
        spread_done = sem("spread_done")
        h_done = sem("h_done")
        down_done = sem("down_done")
        fT_kept = sem("fT_kept")
        f_done = sem("f_done")
        ln4_done = sem("ln4_done")
        fn_done = sem("fn_done")
        fn_last = sem("fn_last")
        ln4_last = sem("ln4_last")
        ot_done = sem("ot_done")
        ot_last = sem("ot_last")
        stored = [sem(f"stored{i}") for i in range(2)]

        N_WQK, N_WA, N_WB = 5, 5, 10
        N_PARTS = 16 * 6
        Y_ALL = NB

        block = ctx.enter_context(nc.Block())

        def x1_bank(i):
            return pX[:, :] if i < 2 else pF[(i - 1) % 2]

        def part3(eng, wait, b):
            wait(part2_done, b + 1)
            eng.tensor_tensor(q_parts[b % 2][:, 2], q_rest[:, :], q_parts[b % 2][:, 1], ALU.subtract)
            eng.tensor_tensor(k_parts[b % 2][:, 2], k_rest[:, :], k_parts[b % 2][:, 1],
                              ALU.subtract).then_inc(part3_done, 1)

        def norm_chain(eng, wait, link, st, work, rs, nm, before_write=None, fused=False):
            v, t, m, d, half = work
            even, odd = st[:, :, 0:3], st[:, :, 3:6]
            eng.tensor_tensor(d, even[:, :, 1], odd[:, :, 1], ALU.subtract)
            eng.tensor_tensor(m, even[:, :, 1], odd[:, :, 1], ALU.add)
            link(eng.tensor_tensor(v, even[:, :, 2], odd[:, :, 2], ALU.add))
            eng.tensor_tensor(d, d, d, ALU.mult)
            eng.tensor_scalar(m, m, -0.5, None, ALU.mult)
            link(eng.tensor_scalar(v, v, 1.0 / D, EPS, ALU.mult, ALU.add))
            link(eng.tensor_scalar(d, d, 0.25, None, ALU.mult))
            link(eng.tensor_tensor(v, v, d, ALU.add))
            if before_write:
                wait(*before_write)
            eng.tensor_scalar(half, v, -0.5, None, ALU.mult)
            link(eng.tensor_scalar(rs.bitcast(I32), v.bitcast(I32), -0.5, float(RSQRT_MAGIC), ALU.mult, ALU.add))
            for _ in range(3):
                link(eng.tensor_tensor(t, rs, rs, ALU.mult))
                link(eng.tensor_tensor(t, t, half, ALU.mult))
                if fused:
                    link(eng.scalar_tensor_tensor(out=rs, in0=t, scalar=1.5, in1=rs, op0=ALU.add, op1=ALU.mult))
                else:
                    link(eng.tensor_scalar(t, t, 1.5, None, ALU.add))
                    link(eng.tensor_tensor(rs, rs, t, ALU.mult))
            return eng.tensor_tensor(nm, m, rs, ALU.mult)

        @block.sync
        def _(sp):
            xd = x.rearrange("(n p) d -> p n d", p=P)
            sp.dma_start(xbig[:, 0:TH], xd[:, 0:TH]).then_inc(xq_loaded[0], 16)
            sp.dma_start(idf[:, :], ident_f).then_inc(wqk_loaded, 16)
            sp.dma_start(wq_sb[:, :], wq).then_inc(wqk_loaded, 16)
            sp.dma_start(wk_sb[:, :], wk).then_inc(wqk_loaded, 16)
            sp.dma_start(bqk_sb[:, 0:1], bq.unsqueeze(1)).then_inc(wqk_loaded, 16)
            sp.dma_start(bqk_sb[:, 1:2], bk.unsqueeze(1)).then_inc(wqk_loaded, 16)
            sp.dma_start(xbig[:, TH:FIRST], xd[:, TH:FIRST]).then_inc(xq_loaded[1], 16)
            sp.dma_start(wv_sb[:, :], wv).then_inc(wa_loaded, 16)
            sp.dma_start(bv_sb[:, :], bv.unsqueeze(0).to_broadcast((P, D))).then_inc(wa_loaded, 16)
            sp.dma_start(idb[:, :], ident_b).then_inc(wa_loaded, 16)
            sp.dma_start(wo_sb[:, :], wo).then_inc(wa_loaded, 16)
            sp.dma_start(bo_sb[:, :], bo.unsqueeze(0).to_broadcast((P, D))).then_inc(wa_loaded, 16)
            sp.dma_start(xbig[:, FIRST:NT], xd[:, FIRST:NT]).then_inc(xq_loaded[2], 16)

            def write_parts(b):
                sp.wait_ge(part3_done, b + 1)
                for parts, which, scratch in ((q_parts[b % 2], Q_PARTS, q_scratch), (k_parts[b % 2], K_PARTS, k_scratch)):
                    s = 0
                    while s < SLOTS:
                        n = 1
                        step = which[s + 1] - which[s] if s + 1 < SLOTS else 0
                        while s + n < SLOTS and step in (0, 1) and which[s + n] - which[s + n - 1] == step:
                            n += 1
                        dst = scratch[b, s:s + n].rearrange("s u d j t -> (u d j) s t")
                        src = (parts[:, which[s]:which[s] + n, :] if n > 1 and step
                               else parts[:, which[s]:which[s] + 1, :].to_broadcast((P, n, T)))
                        sp.dma_start(dst, src).then_inc(scratch_done[b % 2], 16)
                        s += n

            def load_unit(u):
                b, half = divmod(u, 2)
                sp.wait_ge(scratch_done[b % 2], N_PARTS * (b // 2 + 1))
                if u >= RING:
                    sp.wait_ge(s2_done, TH * UB * (u - RING + 1))
                for hh in range(2):
                    rows = slice(QK_ROWS * hh, QK_ROWS * (hh + 1))
                    for dst, scratch in ((qp[u % RING][rows, hh], q_scratch), (kp[u % RING][rows], k_scratch)):
                        sp.dma_start(dst, scratch[b, :, 2 * half + hh].rearrange("s d j t -> s d (j t)")
                                     ).then_inc(packed[u % RING], 16)

            def load_max(u):
                sp.wait_ge(mT_kept, u + 1)
                for hh in range(2):
                    at, n = 2 * QK_ROWS + M_ROWS * hh, M_ROWS * UB
                    sp.dma_start(qp[u % RING][at:at + M_ROWS, hh], mT_sb[u % 2][n * hh:n * (hh + 1), :]
                                 ).then_inc(m_packed[u % RING], 16)

            write_parts(0)
            sp.wait_ge(preset, 1)
            sp.wait_ge(ones_set, 1)
            load_unit(0)
            load_unit(1)
            write_parts(1)
            load_unit(2)
            load_max(0)
            wb = [(h_ring[:, :, :].rearrange("p a (b c) -> p (a b) c", c=P), up),
                  (fT_sb[:, 0:SI].rearrange("p (b c) -> p b c", c=P), shup),
                  (gate_sb[:, :], gate), (down_sb[:, 0:RBLK], down), (down_sb[:, RBLK:FBLK], shdown), (sel_sb[:, :, :], sel)]
            wb += [(ebias_sb[:, c], ebias.unsqueeze(0).to_broadcast((P, E))) for c in range(C4)]
            assert len(wb) == N_WB

            for b in range(NB):
                if 2 * b + 3 < NU:
                    load_unit(2 * b + 3)
                load_max(2 * b + 1)
                if b + 2 < NB:
                    write_parts(b + 2)
                    load_unit(2 * b + 4)
                if b + 1 < NB:
                    load_max(2 * b + 2)
                if 1 <= b <= 3:
                    for dst, src in wb[4 * (b - 1):4 * b]:
                        sp.dma_start(dst, src).then_inc(wb_loaded, 16)

            od = out.rearrange("(n p) d -> p n d", p=P)
            for i in range(NTILE - 1):
                sp.wait_ge(ot_done, i + 1)
                sp.dma_start(od[:, C4 * i:C4 * (i + 1)], ot[i % 2][:, :, :]).then_inc(stored[i % 2], 16)
            for half in range(2):
                sp.wait_ge(ot_last, half + 1)
                c = C4 // 2 * half
                sp.dma_start(od[:, NT - C4 + c:NT - C4 // 2 + c], ot[(NTILE - 1) % 2][:, c:c + C4 // 2]
                             ).then_inc(stored[(NTILE - 1) % 2], 16)
            sp.wait_ge(stored[0], 16 * (NTILE // 2))
            sp.wait_ge(stored[1], 16 * (NTILE // 2 + 1))

        @block.gpsimd
        def _(pool):
            nc.gpsimd.memset(tiny[:, 0:1], 0.0).then_inc(tiny_set, 1)
            for i in range(RING):
                ins = nc.gpsimd.memset(qp[i][:, :, :, :].rearrange("p a b c -> p (a b c)").bitcast(F32), 0.0)
            ins.then_inc(preset, 1)
            nc.gpsimd.memset(m_zero[:, :, :, :], 0.0)
            for i in range(3):
                nc.gpsimd.memset(tied[i][:, :, :], 0.0)
            for i in range(2):
                nc.gpsimd.memset(vv[i][:, :, :, DK + 1:VC], 0.0)
                ins = nc.gpsimd.memset(vv[i][:, :, :, DK:DK + 1], 1.0)
            ins.then_inc(preset, 1)

            def split_max(u):
                pool.wait_ge(max_done, 2 * UB * (u + 1))
                if u >= 1:
                    pool.wait_ge(mT_done, u)
                link = Link(pool, mparts_link, 3 * u)
                m, zero = mneg[u % 2], m_zero[:, :, :, :]
                link(nc.gpsimd.tensor_tensor(m_parts[:, :, :, 0], m[:, :, :, :], zero, ALU.add))
                link(nc.gpsimd.tensor_tensor(m_rest[:, :, :, :], m[:, :, :, :], m_parts[:, :, :, 0], ALU.subtract))
                link(nc.gpsimd.tensor_tensor(m_parts[:, :, :, 1], m_rest[:, :, :, :], zero, ALU.add))
                nc.gpsimd.tensor_tensor(m_parts[:, :, :, 2], m_rest[:, :, :, :], m_parts[:, :, :, 1],
                                        ALU.subtract).then_inc(mparts_done, 1)

            def norm(i, link_sem, stats_sem, st, work, rs, nm, used, ready):
                link = Link(pool, link_sem, LN_LINKS * i)
                pool.wait_ge(stats_sem, i + 1)
                norm_chain(nc.gpsimd, pool.wait_ge, link, st[:, :, :],
                           [w[:, :] for w in work], rs[:, :], nm[:, :],
                           (used, i) if i >= 1 else None).then_inc(ready, 1)
                assert link.n == LN_LINKS

            def chain_y(i):
                norm(i, ln2_link, y_stats, stats2, work2, rs2, nm2, yn_done, ln2_done)

            def chain_x1(i):
                norm(i, ln3_link, x1_stats, stats3, work3, rs3, nm3, xn2_done, ln3_done)

            def chain_f(i):
                norm(i, ln4_link, f_stats, stats4, work4, rs4, nm4, fn_done, ln4_done)

            def residual1(i):
                pool.wait_ge(yn_done, i + 1)
                xi = xbig[:, C4 * i:C4 * (i + 1)]
                nc.gpsimd.tensor_tensor(xi, xi, yn[:, :, :], ALU.add).then_inc(x1_done, 1)

            def residual2(i):
                pool.wait_ge(fn_done, i + 1)
                if i >= 2:
                    pool.wait_ge(stored[i % 2], 16 * (i // 2))
                nc.gpsimd.tensor_tensor(ot[i % 2][:, :, :], xbig[:, C4 * i:C4 * (i + 1)], fn[:, :, :],
                                        ALU.add).then_inc(ot_done, 1)

            for n, (t0, t1) in enumerate(((TH, FIRST), (FIRST, NT))):
                pool.wait_ge(ln1_stats, n + 1)
                norm_chain(nc.gpsimd, pool.wait_ge, Link(pool, ln1_rest_link, LN_LINKS * n), stats[:, t0:t1],
                           [w[:, t0:t1] for w in (nw_v, nw_t, nw_m, nw_d, nw_h)],
                           rs1[:, t0:t1], nm1[:, t0:t1]).then_inc(ln1_rest_done, 1)
            for u in range(NU):
                split_max(u)
                if u % 2 and u // 2 - 1 + AHEAD < NB:
                    part3(nc.gpsimd, pool.wait_ge, u // 2 - 1 + AHEAD)
                for i in range(2):
                    if u == 2 * PREP[i] + 2:
                        chain_y(i)
                    if u == 2 * PREP[i] + 5:
                        residual1(i)
                    if u == 2 * PREP[i] + 6:
                        chain_x1(i)
            chain_y(2)
            for i in range(NTILE):
                if i + 2 < NTILE:
                    residual1(i + 2)
                    chain_x1(i + 2)
                if i >= 1:
                    chain_f(i - 1)
                if i + 3 < NTILE:
                    chain_y(i + 3)
                if i >= 1:
                    residual2(i - 1)

        @block.scalar
        def _(act):
            def normalise(out_, in_, rs, nm):
                return nc.scalar.activation(out_, in_, ACT.Identity, bias=nm, scale=rs)

            def copy(out_, in_):
                return nc.scalar.activation(out_, in_, ACT.Copy)

            def norm_x(b):
                act.wait_ge(*((ln1_done, 1) if b == 0 else (ln1_rest_done, 1 if TH * b < FIRST else 2)))
                if b >= 1:
                    act.wait_ge(xnT_done, b)
                for th in range(TH):
                    t = TH * b + th
                    ins = normalise(xn[:, th], xbig[:, t], rs1[:, t:t + 1], nm1[:, t:t + 1])
                ins.then_inc(xn_done, 1)

            def keep_xnT(b):
                act.wait_ge(xnT_done, b + 1)
                if b >= 2:
                    act.wait_ge(v_done, b - 1)
                copy(xnT[b % 2][:, :], pX[:, 0:T]).then_inc(xnT_kept, 1)

            def part1(b):
                act.wait_ge(qk_done, b + 1)
                if b >= 2:
                    act.wait_ge(scratch_done[b % 2], N_PARTS * (b // 2))
                nc.scalar.activation(q_parts[b % 2][:, 0], pX[:, 0:T], ACT.Identity, bias=bqk_sb[:, 0:1])
                nc.scalar.activation(k_parts[b % 2][:, 0], pX[:, T:2 * T], ACT.Identity,
                                     bias=bqk_sb[:, 1:2]).then_inc(part1_done, 1)

            def part2(b):
                act.wait_ge(rest_done, b + 1)
                copy(q_parts[b % 2][:, 1], q_rest[:, :])
                copy(k_parts[b % 2][:, 1], k_rest[:, :]).then_inc(part2_done, 1)

            def keep_mT(u):
                act.wait_ge(mT_done, u + 1)
                if u >= 2:
                    act.wait_ge(m_packed[(u - 2) % RING], 2 * 16 * ((u - 2) // RING + 1))
                copy(mT_sb[u % 2][:, :], pXb[0:2 * M_ROWS * UB, 0:T]).then_inc(mT_kept, 1)

            def exp(b, j):
                if b >= 1:
                    act.wait_ge(pv_done, 4 * (b - 1) + j // 2 + 1)
                for sh in range(TH):
                    n = TH * (NBLK * b + j) + sh
                    act.wait_ge(s2_done, n + 1)
                    nc.scalar.activation(probs[j][:, sh], pS2[n % S2_RING][:, :, :], ACT.Exp,
                                         scale=SCALE).then_inc(exp_done, 1)

            def keep_oT(b, half):
                act.wait_ge(pv_done, 4 * b + 2 * half + 2)
                if b >= 1:
                    act.wait_ge(o_done, TH * b)
                copy(oT_sb[:, 2 * half:2 * half + 2, :], pO[:, :, :]).then_inc(oT_kept, 1)

            def keep_onT(b):
                act.wait_ge(onT_done, b + 1)
                if b >= 1:
                    act.wait_ge(y_done, b)
                copy(onT[:, :], pY[:, 0:T]).then_inc(onT_kept, 1)

            def norm_y(i, c):
                if c == 0:
                    act.wait_ge(ln2_done, i + 1)
                    if i >= 1:
                        act.wait_ge(x1_done, i)
                ins = normalise(yn[:, c], ybig[:, C4 * i + c], rs2[:, c:c + 1], nm2[:, c:c + 1])
                if c == C4 - 1:
                    ins.then_inc(yn_done, 1)

            def norm_x1(i, c):
                if c == 0:
                    act.wait_ge(ln3_done, i + 1)
                    if i >= 1:
                        act.wait_ge(x2T_done, i)
                ins = normalise(xn2[:, c], xbig[:, C4 * i + c], rs3[:, c:c + 1], nm3[:, c:c + 1])
                if c == C4 - 1:
                    ins.then_inc(xn2_done, 1)

            def keep_xT(i):
                act.wait_ge(x2T_done, i + 1)
                if i >= 1:
                    act.wait_ge(logit_done, i)
                    act.wait_ge(xlo_done, i)
                copy(xT[:, :], x1_bank(i)).then_inc(xT_kept, 1)

            def high_x(i):
                act.wait_ge(xcut_done, i + 1)
                if i >= 2:
                    act.wait_ge(up_done, FBLK * (i - 1))
                copy(x_hi[i % 2], x_cut).then_inc(xhi_done, 1)

            def high_up(c):
                act.wait_ge(wcut_done, c + 1)
                blocks = slice(CUT * c, min(CUT * (c + 1), FBLK))
                copy(up_hi[:, blocks].rearrange("p a b -> p (a b)"),
                     w_cut[:, 0:P * (blocks.stop - blocks.start)]).then_inc(whi_done, 1)

            def exp_logits(i):
                act.wait_ge(logit_done, i + 1)
                if i >= 1:
                    act.wait_ge(cparts_done, i)
                nc.scalar.activation(e_sb[:, :, :], pX[:, 0:C4 * E], ACT.Exp, scale=-1.0).then_inc(e_done, 1)

            def keep_cT(i):
                act.wait_ge(cT_done, i + 1)
                if i >= 2:
                    act.wait_ge(spread_done, RBLK * (i - 1))
                copy(cT[i % 2][:, :], pXb[0:3 * E, 0:TILE]).then_inc(cT_kept, 1)

            def relu_square(i, k):
                n = FBLK * i + k
                act.wait_ge(up_done, n + 1)
                nc.scalar.activation(r_sb[k % 2][:, :], pU[k % 2], ACT.Relu).then_inc(relu_done, 1)
                act.wait_ge(relu_done, n + 1)
                if k < RBLK:
                    if RBLK * i + k >= 2:
                        act.wait_ge(h_done, RBLK * i + k - 1)
                    dst = r2_sb[k % 2][:, :]
                else:
                    act.wait_ge(down_done, n - HRING + 1)
                    dst = h_sb[n % HRING]
                nc.scalar.activation(dst, r_sb[k % 2][:, :], ACT.Square).then_inc(sq_done, 1)

            def keep_fT(i):
                act.wait_ge(down_done, FBLK * (i + 1))
                if i >= 1:
                    act.wait_ge(f_done, i)
                copy(fT_sb[:, :], pF[i % 2]).then_inc(fT_kept, 1)

            def norm_f(i, c):
                if c == 0:
                    act.wait_ge(ln4_done, i + 1)
                    if i >= 1:
                        act.wait_ge(ot_done, i)
                ins = normalise(fn[:, c], pN[:, D * c:D * (c + 1)], rs4[:, c:c + 1], nm4[:, c:c + 1])
                if i == NTILE - 1:
                    ins.then_inc(fn_last, 1)
                elif c == C4 - 1:
                    ins.then_inc(fn_done, 1)

            act.wait_ge(tiny_set, 1)
            nc.scalar.activation(tiny[:, 1:2], tiny[:, 0:1], ACT.Exp)
            act.wait_ge(wqk_loaded, 16 * N_WQK)
            act.wait_ge(xq_loaded[0], 16)
            for b in range(AHEAD):
                if b == 1:
                    act.wait_ge(xq_loaded[1], 16)
                norm_x(b)
                keep_xnT(b)
                part1(b)
                if b + 1 < AHEAD:
                    part2(b)
            keep_mT(0)
            act.wait_ge(xq_loaded[2], 16)

            for b in range(NB):
                proj = b + AHEAD < NB
                for j in range(NBLK):
                    exp(b, j)
                    if j == 0:
                        if b - 1 + AHEAD < NB:
                            part2(b - 1 + AHEAD)
                        keep_mT(2 * b + 1)
                    if j == 1 and b >= 1:
                        keep_oT(b - 1, 1)
                    if j == 2 and proj:
                        norm_x(b + AHEAD)
                    if j == 3 and b == NB - 4:
                        keep_xT(0)
                    if j == 7 and CUT_BATCH <= b < CUT_BATCH + NCUT:
                        high_up(b - CUT_BATCH)
                    if j == 7 and b == NB - 1:
                        high_x(0)
                    if j == 4:
                        if proj:
                            keep_xnT(b + AHEAD)
                        if b >= 1:
                            keep_onT(b - 1)
                    if j == 5:
                        if b + 1 < NB:
                            keep_mT(2 * b + 2)
                        keep_oT(b, 0)
                    if j == 6 and proj:
                        part1(b + AHEAD)
                    if j == 1 and b == NB - 3:
                        exp_logits(0)
                    if b - 1 in PREP and j % 2:
                        norm_y(PREP.index(b - 1), j // 2)
                    if b == PREP[0] + 3 and j % 2:
                        norm_x1(0, j // 2)
                    if b == NB - 3 and j >= C4:
                        norm_x1(1, j - C4)
            keep_cT(0)
            for i in range(NTILE):
                for k in range(FBLK):
                    relu_square(i, k)
                    if i == 0:
                        if k == 0:
                            keep_oT(NB - 1, 1)
                        if k == 7:
                            keep_onT(NB - 1)
                    if i == 0 and k == 1:
                        keep_xT(1)
                    if i + 1 < NTILE:
                        if k == (2 if i == 0 else 0):
                            exp_logits(i + 1)
                        if k == 15:
                            high_x(i + 1)
                        if k == 16:
                            keep_cT(i + 1)
                    if i + 2 < NTILE:
                        if k in NORM_Y_AT[i >= 1]:
                            norm_y(i + 2, NORM_Y_AT[i >= 1].index(k))
                        if k in NORM_X1_AT[i >= 1]:
                            norm_x1(i + 2, NORM_X1_AT[i >= 1].index(k))
                        if k == 17 - (i >= 1):
                            keep_xT(i + 2)
                    if i >= 1:
                        if k == 2:
                            keep_fT(i - 1)
                        if 14 <= k < 14 + C4:
                            norm_f(i - 1, k - 14)
            keep_fT(NTILE - 1)
            for c in range(C4):
                norm_f(NTILE - 1, c)

        @block.vector
        def _(dve):
            def rest(b):
                dve.wait_ge(part1_done, b + 1)
                if b >= 1:
                    dve.wait_ge(part3_done, b)
                for i, (left, parts) in enumerate(((q_rest, q_parts[b % 2]), (k_rest, k_parts[b % 2]))):
                    ins = nc.vector.scalar_tensor_tensor(out=left[:, :], in0=pX[:, T * i:T * (i + 1)],
                                                         scalar=bqk_sb[:, i:i + 1], in1=parts[:, 0],
                                                         op0=ALU.add, op1=ALU.subtract)
                ins.then_inc(rest_done, 1)

            def keep_v(b):
                dve.wait_ge(v_done, b + 1)
                if b >= 2:
                    dve.wait_ge(pv_done, 4 * (b - 1))
                nc.vector.tensor_tensor(vv[b % 2][:, :, :, 0:DK],
                                        pY[:, 0:T].rearrange("p (a h d) -> p a h d", a=TH, h=H),
                                        bv_sb[:, :].rearrange("p (h d) -> p h d", h=H).unsqueeze(1)
                                        .to_broadcast((P, TH, H, DK)),
                                        ALU.add).then_inc(v_kept, 1)

            def row_max(u, k):
                if k == 0 and u >= 2:
                    dve.wait_ge(mparts_done, u - 1)
                for hh in range(2):
                    n = 2 * (UB * u + k) + hh
                    dve.wait_ge(s1_done, n + 1)
                    nc.vector.tensor_reduce(mneg[u % 2][:, :, hh, k], pS1[n % S1_RING][:, :].rearrange("p (a s) -> p a s", a=TH),
                                            AX.X, ALU.max, negate=True).then_inc(max_done, 1)

            def norm_o(b, th):
                dve.wait_ge(o_done, TH * b + th + 1)
                o = (pX, pY)[th][:, :].rearrange("p (h c) -> p h c", c=VC)
                nc.vector.reciprocal(o_rec[:, th], o[:, :, DK]).then_inc(rec_done, 1)
                dve.wait_ge(rec_done, TH * b + th + 1)
                if b >= 1:
                    dve.wait_ge(onT_done, b)
                nc.vector.tensor_tensor(o_sb[:, th].rearrange("p (h d) -> p h d", h=H), o[:, :, 0:DK],
                                        o_rec[:, th].unsqueeze(2).to_broadcast((P, H, DK)),
                                        ALU.mult).then_inc(o_kept, 1)

            def keep_y(b):
                dve.wait_ge(y_done, b + 1)
                nc.vector.tensor_tensor(ybig[:, TH * b:TH * (b + 1)],
                                        pY[:, 0:T].rearrange("p (a e) -> p a e", a=TH),
                                        bo_sb[:, :].unsqueeze(1).to_broadcast((P, TH, D)),
                                        ALU.add).then_inc(y_kept, 1)

            def stats_y(i):
                dve.wait_ge(y_kept, 2 * (i + 1))
                if i >= 1:
                    dve.wait_ge(ln2_done, i)
                for c in range(C4):
                    ins = nc.vector.bn_stats(stats2[:, c, :], ybig[:, C4 * i + c])
                ins.then_inc(y_stats, 1)

            def stats_x1(i):
                dve.wait_ge(x1_done, i + 1)
                if i >= 1:
                    dve.wait_ge(ln3_done, i)
                for c in range(C4):
                    ins = nc.vector.bn_stats(stats3[:, c, :], xbig[:, C4 * i + c])
                ins.then_inc(x1_stats, 1)

            def stats_f(i):
                dve.wait_ge(f_done, i + 1)
                if i >= 1:
                    dve.wait_ge(ln4_done, i)
                for c in range(C4):
                    ins = nc.vector.bn_stats(stats4[:, c, :], pN[:, D * c:D * (c + 1)])
                ins.then_inc(f_stats, 1)

            PAD = E // 2
            flat = lambda i, n, s=0: tied[i][:, :, PAD - s:PAD - s + n]

            def pick_ties(link, values, n, at):
                least = top8[:, :, at - 1:at].to_broadcast((P, C4, n))
                nc.vector.tensor_tensor(above[:, :, 0:n], values, least, ALU.is_gt)
                link(nc.vector.tensor_tensor(flat(0, n), values, least, ALU.is_equal))

            def pick_need(link, n, want):
                link(nc.vector.tensor_reduce(need[:, :], above[:, :, 0:n], AX.X, ALU.add))
                link(nc.vector.tensor_scalar(need[:, :], need[:, :], -1.0, float(want), ALU.mult, ALU.add))

            def pick_prefix(link, n, steps):
                for s in steps:
                    src, dst = 0 if s == 0 else 2 - s % 2, 1 + s % 2
                    link(nc.vector.tensor_tensor(flat(dst, n), flat(src, n), flat(src, n, 1 << s), ALU.add))

            def pick_fill(link, n, steps, picked_):
                src = 2 - steps % 2
                link(nc.vector.tensor_tensor(picked_, flat(src, n), need[:, :].unsqueeze(2).to_broadcast((P, C4, n)),
                                             ALU.is_le))
                link(nc.vector.tensor_tensor(picked_, picked_, flat(0, n), ALU.mult))
                link(nc.vector.tensor_tensor(picked_, picked_, above[:, :, 0:n], ALU.add))

            def route(link, i, step):
                g = choice[:, :, :].rearrange("p c (g m) -> p (c g) m", g=GROUPS)
                if step == 0:
                    dve.wait_ge(e_done, i + 1)
                    link(nc.vector.tensor_scalar(score[:, :, :], e_sb[:, :, :], 1.0, None, ALU.add))
                    link(nc.vector.reciprocal(score[:, :, :], score[:, :, :]))
                if step == 1:
                    link(nc.vector.tensor_tensor(choice[:, :, :], score[:, :, :], ebias_sb[:, :, :], ALU.add))
                    nc.vector.tensor_tensor(pair_hi[:, :, :], g[:, :, 0:2], g[:, :, 2:4], ALU.max)
                    link(nc.vector.tensor_tensor(pair_lo[:, :, :], g[:, :, 0:2], g[:, :, 2:4], ALU.min))
                    nc.vector.tensor_tensor(g_top[:, :], pair_hi[:, :, 0], pair_hi[:, :, 1], ALU.max)
                    nc.vector.tensor_tensor(g_mid[:, :], pair_hi[:, :, 0], pair_hi[:, :, 1], ALU.min)
                    link(nc.vector.tensor_tensor(g_low[:, :], pair_lo[:, :, 0], pair_lo[:, :, 1], ALU.max))
                if step == 2:
                    link(nc.vector.tensor_tensor(g_mid[:, :], g_mid[:, :], g_low[:, :], ALU.max))
                    link(nc.vector.tensor_tensor(g_score[:, :, :].rearrange("p c g -> p (c g)"), g_top[:, :],
                                                 g_mid[:, :], ALU.add))
                    for c in range(C4):
                        ins = nc.vector.max(top8[:, c], g_score[:, c])
                    link(ins)
                if step == 3:
                    pick_ties(link, g_score[:, :, :], GROUPS, TOPG)
                    pick_need(link, GROUPS, TOPG)
                    pick_prefix(link, GROUPS, (0,))
                if step == 4:
                    pick_prefix(link, GROUPS, (1, 2))
                    pick_fill(link, GROUPS, 3, picked_g[:, :, :])
                if step == 5:
                    link(nc.vector.tensor_tensor(g, g, picked_g[:, :, :].rearrange("p c g -> p (c g)").unsqueeze(2)
                                                 .to_broadcast((P, C4 * GROUPS, E // GROUPS)), ALU.mult))
                    for c in range(C4):
                        ins = nc.vector.max(top8[:, c], choice[:, c])
                    link(ins)
                if step == 6:
                    pick_ties(link, choice[:, :, :], E, TOPK)
                    pick_need(link, E, TOPK)
                if step == 7:
                    pick_prefix(link, E, (0, 1, 2))
                if step == 8:
                    pick_prefix(link, E, (3, 4))
                if step == 9:
                    pick_fill(link, E, 5, picked[:, :, :])
                if step == 10:
                    link(nc.vector.tensor_tensor(comb[:, :, :], score[:, :, :], picked[:, :, :], ALU.mult))
                    link(nc.vector.tensor_reduce(w_sum[:, :], comb[:, :, :], AX.X, ALU.add))
                    link(nc.vector.tensor_scalar(w_sum[:, :], w_sum[:, :], 1e-20, None, ALU.add))
                    link(nc.vector.reciprocal(w_sum[:, :], w_sum[:, :]))
                if step == 11:
                    link(nc.vector.scalar_tensor_tensor(out=comb[:, :, :], in0=comb[:, :, :], scalar=ROUTED_SCALE,
                                                        in1=w_sum[:, :].unsqueeze(2).to_broadcast((P, C4, E)),
                                                        op0=ALU.mult, op1=ALU.mult))
                    if i >= 1:
                        dve.wait_ge(cT_done, i)
                    link(nc.vector.tensor_copy(c_parts[:, :, 0], comb[:, :, :]))
                    link(nc.vector.tensor_tensor(c_rest[:, :, :], comb[:, :, :], c_parts[:, :, 0], ALU.subtract))
                    link(nc.vector.tensor_copy(c_parts[:, :, 1], c_rest[:, :, :]))
                    nc.vector.tensor_tensor(c_parts[:, :, 2], c_rest[:, :, :], c_parts[:, :, 1],
                                            ALU.subtract).then_inc(cparts_done, 1)
                    assert link.n == RT_LINKS, link.n

            def cut_x(i):
                dve.wait_ge(xT_kept, i + 1)
                if i >= 1:
                    dve.wait_ge(xhi_done, i)
                    dve.wait_ge(xlo_done, i)
                else:
                    dve.wait_ge(s2_done, TH * NBLK * (NB - 1))
                nc.vector.tensor_scalar(x_cut.bitcast(I32), xT[:, :].bitcast(I32), HIGH_MASK, None,
                                        ALU.bitwise_and).then_inc(xcut_done, 1)
                dve.wait_ge(xcut_done, i + 1)
                if i >= 2:
                    dve.wait_ge(up_done, FBLK * (i - 1))
                nc.vector.tensor_tensor(x_lo[i % 2], xT[:, :], x_cut, ALU.subtract).then_inc(xlo_done, 1)

            def cut_up(c):
                if c == 0:
                    dve.wait_ge(wb_loaded, 16 * N_WB)
                else:
                    dve.wait_ge(whi_done, c)
                    dve.wait_ge(wlo_done, c)
                blocks = slice(CUT * c, min(CUT * (c + 1), FBLK))
                bits = w_cut[:, 0:P * (blocks.stop - blocks.start)]
                nc.vector.tensor_scalar(bits.bitcast(I32), up_in[c].bitcast(I32), HIGH_MASK, None,
                                        ALU.bitwise_and).then_inc(wcut_done, 1)
                dve.wait_ge(wcut_done, c + 1)
                nc.vector.tensor_tensor(up_lo[:, blocks].rearrange("p a b -> p (a b)"), up_in[c], bits,
                                        ALU.subtract).then_inc(wlo_done, 1)

            def weigh(i, k):
                n = FBLK * i + k
                dve.wait_ge(sq_done, n + 1)
                dve.wait_ge(spread_done, RBLK * i + k + 1)
                if n >= HRING:
                    dve.wait_ge(down_done, n - HRING + 1)
                if n == 0:
                    dve.wait_ge(wlo_done, NCUT)
                nc.vector.tensor_tensor(h_sb[n % HRING], pC[k % 2], r2_sb[k % 2][:, :],
                                        ALU.mult).then_inc(h_done, 1)

            link = Link(dve, ln1_link, 0)
            for i in range(RING - 1):
                nc.vector.memset(kp[i][2 * QK_ROWS:P, :, :], 1.0)
            dve.wait_ge(xq_loaded[0], 16)
            for t in range(TH):
                ins = nc.vector.bn_stats(stats[:, t, :], xbig[:, t])
            link(ins)
            norm_chain(nc.vector, dve.wait_ge, link, stats[:, 0:TH],
                       [w[:, 0:TH] for w in (nw_v, nw_t, nw_m, nw_d, nw_h)],
                       rs1[:, 0:TH], nm1[:, 0:TH], fused=True).then_inc(ln1_done, 1)
            dve.wait_ge(xq_loaded[1], 16)
            for t in range(TH, FIRST):
                ins = nc.vector.bn_stats(stats[:, t, :], xbig[:, t])
            ins.then_inc(ln1_stats, 1)
            nc.vector.memset(kp[RING - 1][2 * QK_ROWS:P, :, :], 1.0).then_inc(ones_set, 1)
            dve.wait_ge(wqk_loaded, 16 * N_WQK)
            rest(0)
            part3(nc.vector, dve.wait_ge, 0)
            dve.wait_ge(wa_loaded, 16 * N_WA)
            dve.wait_ge(preset, 2)
            keep_v(0)
            dve.wait_ge(xq_loaded[2], 16)
            for t in range(FIRST, FIRST + NT // 3):
                nc.vector.bn_stats(stats[:, t, :], xbig[:, t])
            rest(1)
            part3(nc.vector, dve.wait_ge, 1)
            for t in range(FIRST + NT // 3, NT):
                ins = nc.vector.bn_stats(stats[:, t, :], xbig[:, t])
            ins.then_inc(ln1_stats, 1)
            rest(2)
            for u in range(2):
                for k in range(UB):
                    row_max(u, k)

            rt = Link(dve, rt_link, 0)
            for b in range(NB):
                last = b == NB - 1
                for j in range(NBLK):
                    if b + 1 < NB:
                        row_max(2 * b + 2 + j // UB, j % UB)
                    if j == 1 and b + 1 < NB:
                        keep_v(b + 1)
                    if j in (2, 3) and b >= 1:
                        norm_o(b - 1, j - 2)
                    if j == 6 and b >= 1:
                        keep_y(b - 1)
                    if j == 7 and b + AHEAD < NB:
                        rest(b + AHEAD)
                    if j == 5 and CUT_BATCH <= b < CUT_BATCH + NCUT:
                        cut_up(b - CUT_BATCH)
                    if last and j == 0:
                        cut_x(0)
                    if b in PREP and j == 4:
                        stats_y(PREP.index(b))
                    if b - 2 in PREP and j == 4:
                        stats_x1(PREP.index(b - 2))
                    if b >= NB - 3:
                        for step in ROUTE_FIRST[b - (NB - 3)][j]:
                            route(rt, 0, step)

            for i in range(NTILE):
                rt = Link(dve, rt_link, RT_LINKS * (i + 1))
                for k in range(RBLK):
                    weigh(i, k)
                    if i == 0:
                        if k in (4, 5):
                            norm_o(NB - 1, k - 4)
                        if k == 10:
                            keep_y(NB - 1)
                    if i + 1 < NTILE and k in ROUTE_AT[i >= 1]:
                        route(rt, i + 1, ROUTE_AT[i >= 1].index(k))
                    if i + 1 < NTILE and k == 14:
                        cut_x(i + 1)
                    if i == 0 and k == 0:
                        stats_y(2)
                    if i + 3 < NTILE and k == 15:
                        stats_y(i + 3)
                    if i + 2 < NTILE:
                        if k == 7:
                            stats_x1(i + 2)
                    if i >= 1 and k == 10:
                        stats_f(i - 1)
            stats_f(NTILE - 1)
            dve.wait_ge(f_stats, NTILE)
            norm_chain(nc.vector, dve.wait_ge, Link(dve, ln4_last, 0), stats4[:, :, :], [w[:, :] for w in work4],
                       rs4[:, :], nm4[:, :], (fn_done, NTILE - 1), fused=True).then_inc(ln4_done, 1)
            for half in range(2):
                dve.wait_ge(fn_last, C4 // 2 * (half + 1))
                if half == 0:
                    dve.wait_ge(stored[(NTILE - 1) % 2], 16 * (NTILE // 2 - 1))
                cs = slice(C4 // 2 * half, C4 // 2 * (half + 1))
                nc.vector.tensor_tensor(ot[(NTILE - 1) % 2][:, cs], fn[:, cs],
                                        xbig[:, NT - C4 + cs.start:NT - C4 + cs.stop], ALU.add).then_inc(ot_last, 1)

        @block.tensor
        def _(pe):
            mm, tr = nc.tensor.matmul, nc.tensor.transpose

            def transpose_x(b):
                pe.wait_ge(xn_done, b + 1)
                for th in range(TH):
                    ins = tr(pX[:, P * th:P * (th + 1)], xn[:, th], idf[:, :])
                ins.then_inc(xnT_done, 1)

            def project_qk(b):
                pe.wait_ge(xnT_kept, b + 1)
                mm(pX[:, 0:T], wq_sb[:, :], xnT[b % 2][:, :], start=True, stop=True)
                mm(pX[:, T:2 * T], wk_sb[:, :], xnT[b % 2][:, :], start=True, stop=True).then_inc(qk_done, 1)

            def project_v(b):
                pe.wait_ge(xnT_kept, b + 1)
                for th in range(TH):
                    ins = mm(pY[:, D * th:D * (th + 1)], xnT[b % 2][:, P * th:P * (th + 1)], wv_sb[:, :],
                             start=True, stop=True)
                ins.then_inc(v_done, 1)

            def scores_by_query(u, k, hh):
                slot, n = u % RING, 2 * (UB * u + k) + hh
                if k == 0 and hh == 0:
                    pe.wait_ge(packed[slot], 4 * 16 * (u // RING + 1))
                if n >= S1_RING:
                    pe.wait_ge(max_done, n - S1_RING + 1)
                for th in range(TH):
                    ins = mm(pS1[n % S1_RING][:, T * th:T * (th + 1)], qp[slot][0:2 * QK_ROWS, hh, k, P * th:P * (th + 1)],
                             kp[slot][0:2 * QK_ROWS, k, :], start=True, stop=True)
                ins.then_inc(s1_done, 1)

            def scores_by_key(b, j, sh):
                u, k = 2 * b + j // UB, j % UB
                slot, n = u % RING, TH * (NBLK * b + j) + sh
                if k == 0 and sh == 0:
                    pe.wait_ge(m_packed[slot], 2 * 16 * (u // RING + 1))
                if n >= S2_RING:
                    pe.wait_ge(exp_done, n - S2_RING + 1)
                mm(pS2[n % S2_RING][:, :, :], kp[slot][0:DIFF_ROWS, k, P * sh:P * (sh + 1)],
                   qp[slot][0:DIFF_ROWS, :, k, :], start=True, stop=True).then_inc(s2_done, 1)

            def outputs(b, g):
                pe.wait_ge(exp_done, TH * (NBLK * b + 2 * g + 2))
                if g == 0:
                    pe.wait_ge(v_kept, b + 1)
                if g % 2 == 0 and 2 * b + g // 2 >= 1:
                    pe.wait_ge(oT_kept, 2 * b + g // 2)
                for sh in range(TH):
                    for h in range(4):
                        ins = mm(pO[VC * h:VC * (h + 1), g % 2], vv[b % 2][:, sh, 4 * g + h, :],
                                 probs[2 * g + h // 2][:, sh, h % 2, :], start=sh == 0, stop=sh == TH - 1)
                ins.then_inc(pv_done, 1)

            def transpose_max(u):
                pe.wait_ge(mparts_done, u + 1)
                for th in range(TH):
                    ins = tr(pXb[0:2 * M_ROWS * UB, P * th:P * (th + 1)],
                             m_parts[:, th].rearrange("p a b c -> p (a b c)"), idb[:, :])
                ins.then_inc(mT_done, 1)

            def transpose_o(b, th):
                pe.wait_ge(oT_kept, 2 * b + 2)
                for g in range(4):
                    ins = tr((pX, pY)[th][:, P * g:P * (g + 1)], oT_sb[:, g, P * th:P * (th + 1)], idf[:, :])
                ins.then_inc(o_done, 1)

            def transpose_on(b):
                pe.wait_ge(o_kept, TH * (b + 1))
                for th in range(TH):
                    ins = tr(pY[:, P * th:P * (th + 1)], o_sb[:, th], idf[:, :])
                ins.then_inc(onT_done, 1)

            def project_y(b):
                pe.wait_ge(onT_kept, b + 1)
                for th in range(TH):
                    ins = mm(pY[:, D * th:D * (th + 1)], onT[:, P * th:P * (th + 1)], wo_sb[:, :],
                             start=True, stop=True)
                ins.then_inc(y_done, 1)

            def transpose_x1(i):
                pe.wait_ge(xn2_done, i + 1)
                for c in range(C4):
                    ins = tr(x1_bank(i)[:, P * c:P * (c + 1)], xn2[:, c], idf[:, :])
                ins.then_inc(x2T_done, 1)

            def logits(i):
                pe.wait_ge(xT_kept, i + 1)
                for c in range(C4):
                    ins = mm(pX[:, E * c:E * (c + 1)], xT[:, P * c:P * (c + 1)], gate_sb[:, :],
                             start=True, stop=True)
                ins.then_inc(logit_done, 1)

            def transpose_c(i):
                pe.wait_ge(cparts_done, i + 1)
                for c in range(C4):
                    ins = tr(pXb[0:3 * E, P * c:P * (c + 1)], c_parts[:, c].rearrange("p a e -> p (a e)"), idb[:, :])
                ins.then_inc(cT_done, 1)

            def up_block(i, k):
                n = FBLK * i + k
                if n >= 2:
                    pe.wait_ge(relu_done, n - 1)
                if k == 0:
                    pe.wait_ge(xhi_done, i + 1)
                    pe.wait_ge(xlo_done, i + 1)
                if n == 0:
                    pe.wait_ge(whi_done, NCUT)
                    pe.wait_ge(wlo_done, NCUT)
                mm(pU[k % 2], up_hi[:, k], x_hi[i % 2], start=True, stop=False)
                mm(pU[k % 2], up_hi[:, k], x_lo[i % 2], start=False, stop=False)
                mm(pU[k % 2], up_lo[:, k], x_hi[i % 2], start=False, stop=True).then_inc(up_done, 1)

            def spread_block(i, k):
                if k == 0:
                    pe.wait_ge(cT_kept, i + 1)
                if RBLK * i + k >= 2:
                    pe.wait_ge(h_done, RBLK * i + k - 1)
                mm(pC[k % 2], sel_sb[:, k], cT[i % 2][:, :], start=True, stop=True).then_inc(spread_done, 1)

            def down_block(n):
                i, k = divmod(n, FBLK)
                if k < RBLK:
                    pe.wait_ge(h_done, RBLK * i + k + 1)
                else:
                    pe.wait_ge(sq_done, n + 1)
                if k == 0 and i >= 2:
                    pe.wait_ge(fT_kept, i - 1)
                if k == 0 and 1 <= i < NTILE - 1:
                    pe.wait_ge(xT_kept, i + 2)
                if k == 0 and i == 1:
                    pe.wait_ge(y_kept, NB)
                mm(pF[i % 2], down_sb[:, k], h_sb[n % HRING], start=k == 0,
                   stop=k == FBLK - 1).then_inc(down_done, 1)

            def transpose_f(i):
                pe.wait_ge(fT_kept, i + 1)
                if i >= 1:
                    pe.wait_ge(fn_done, i)
                for c in range(C4):
                    ins = tr(pN[:, P * c:P * (c + 1)], fT_sb[:, P * c:P * (c + 1)], idf[:, :])
                ins.then_inc(f_done, 1)

            pe.wait_ge(wqk_loaded, 16 * N_WQK)
            for b in range(AHEAD):
                if b >= 1:
                    pe.wait_ge(rest_done, b)
                transpose_x(b)
                project_qk(b)
                if b == 0:
                    pe.wait_ge(wa_loaded, 16 * N_WA)
                    project_v(0)
            for u in range(2):
                for k in range(UB):
                    for hh in range(2):
                        scores_by_query(u, k, hh)
                    if u == 1 and k == 1:
                        pe.wait_ge(rest_done, AHEAD)
                        transpose_max(0)

            for b in range(NB):
                proj = b + AHEAD < NB
                last = b == NB - 1
                for j in range(NBLK):
                    for hh in range(2):
                        if not last:
                            scores_by_query(2 * b + 2 + j // UB, j % UB, hh)
                        scores_by_key(b, j, hh)
                        if j == 1 and hh == 0:
                            if b - 1 + AHEAD < NB:
                                pe.wait_ge(rest_done, b + AHEAD)
                            else:
                                pe.wait_ge(mT_kept, 2 * b + 1)
                            transpose_max(2 * b + 1)
                        if j == 6 and hh == 0 and proj:
                            pe.wait_ge(mT_kept, 2 * b + 3)
                            project_qk(b + AHEAD)
                    if j == 1:
                        if b >= 1:
                            outputs(b - 1, 3)
                        if not last:
                            if b >= 2:
                                pe.wait_ge(y_kept, b - 1)
                            project_v(b + 1)
                    if j == 1 and b == NB - 3:
                        pe.wait_ge(mT_kept, 2 * b + 2)
                        pe.wait_ge(wb_loaded, 16 * N_WB)
                        logits(0)
                    if j == 2 and b >= 1:
                        pe.wait_ge(*((e_done, 1) if b == NB - 3 else (mT_kept, 2 * b + 2)))
                        transpose_o(b - 1, 0)
                    if j == 3:
                        if b >= 1:
                            pe.wait_ge(*((y_kept, b - 1) if last else (v_kept, b + 2)))
                            transpose_o(b - 1, 1)
                        outputs(b, 0)
                    if j == 3 and b == NB - 4:
                        pe.wait_ge(o_kept, TH * (b - 1) + 1)
                        transpose_x1(0)
                    if j == 4:
                        pe.wait_ge(*((xT_kept, 1) if b == NB - 4 else
                                     (o_kept, TH * (b - 1) + 1) if b >= 1 else (mT_kept, 2)))
                        if proj:
                            transpose_x(b + AHEAD)
                        if b >= 1:
                            transpose_on(b - 1)
                    if j == 5:
                        if not last:
                            if proj:
                                pe.wait_ge(xnT_kept, b + AHEAD + 1)
                            transpose_max(2 * b + 2)
                        if b >= 1:
                            project_y(b - 1)
                        outputs(b, 1)
                    if j == 7:
                        outputs(b, 2)
                        if last:
                            transpose_c(0)

            pe.wait_ge(max_done, H * NB)
            pe.wait_ge(exp_done, TH * NBLK * NB)
            for i in range(NTILE):
                for k in range(FBLK):
                    n = FBLK * i + k
                    up_block(i, k)
                    if n >= LAG:
                        down_block(n - LAG)
                    if k < RBLK:
                        spread_block(i, k)
                    if i == 0 and k == 0:
                        outputs(NB - 1, 3)
                    if i == 0:
                        if k == 4:
                            pe.wait_ge(e_done, 2)
                            transpose_o(NB - 1, 0)
                        if k == 5:
                            pe.wait_ge(y_kept, NB - 1)
                            transpose_o(NB - 1, 1)
                        if k == 7:
                            transpose_on(NB - 1)
                        if k == 9:
                            project_y(NB - 1)
                    elif k == 4:
                        pe.wait_ge(oT_kept, 2 * NB)
                        transpose_f(i - 1)
                    if i + 1 < NTILE:
                        if i == 0 and k == 1:
                            pe.wait_ge(cT_kept, 1)
                            transpose_x1(1)
                        if k == (2 if i == 0 else 0):
                            logits(i + 1)
                        if k == 16:
                            transpose_c(i + 1)
                        if k == 17 - (i >= 1) and i + 2 < NTILE:
                            pe.wait_ge(*((fT_kept, i) if i >= 1 else (y_kept, NB)))
                            transpose_x1(i + 2)
            for n in range(FBLK * NTILE - LAG, FBLK * NTILE):
                down_block(n)
            transpose_f(NTILE - 1)


def kernel(**inputs):
    import ml_dtypes
    import concourse.bacc as bacc
    from concourse.bass_utils import run_bass_kernel_spmd

    a = {k: np.asarray(v) for k, v in inputs.items()}
    order = lambda w: w.reshape((2, UB, 2, DK) + w.shape[1:]).transpose(
        (0, 2, 3, 1) + tuple(range(4, 3 + w.ndim))).reshape(w.shape)
    names = ["x", "wq", "wk", "wv", "wo", "bq", "bk", "bv", "bo", "gate", "ebias", "up", "shup", "down", "shdown",
             "ident_f", "ident_b", "sel"]
    sel = np.zeros((3, E, RBLK, P), ml_dtypes.bfloat16)
    for e in range(E):
        blk, at = divmod(e * EI, P)
        sel[:, e, blk, at:at + EI] = 1
    arrays = {
        "x": a["L0_attn_x"].reshape(NB * T, D),
        "wq": order(a["L0_attn_w_q"]).T,
        "wk": order(a["L0_attn_w_k"]).T,
        "wv": a["L0_attn_w_v"].T,
        "wo": a["L0_attn_w_o"].T,
        "bq": order(a["L0_attn_b_q"]),
        "bk": order(a["L0_attn_b_k"]),
        "bv": a["L0_attn_b_v"],
        "bo": a["L0_attn_b_o"],
        "gate": a["L0_ffn_gate_w"].T,
        "ebias": a["L0_ffn_e_bias"],
        "up": a["L0_ffn_up_w"].reshape(RBLK, P, D).transpose(2, 0, 1),
        "shup": a["L0_ffn_shared_up_w"].reshape(SI // P, P, D).transpose(2, 0, 1),
        "down": a["L0_ffn_down_w"].reshape(RBLK, P // EI, D, EI).transpose(1, 3, 0, 2).reshape(P, RBLK, D),
        "shdown": a["L0_ffn_shared_down_w"].reshape(D, SI // P, P).transpose(2, 1, 0),
        "ident_f": np.eye(P, dtype=np.float32),
        "ident_b": np.eye(P, dtype=ml_dtypes.bfloat16),
        "sel": sel.reshape(3 * E, RBLK, P),
    }
    nc = bacc.Bacc("TRN2", target_bir_lowering=False, num_devices=1)
    args, maps = [], {}
    for name in names:
        v = np.ascontiguousarray(arrays[name])
        maps[f"in_{name}"] = v
        args.append(nc.dram_tensor(f"in_{name}", v.shape, mybir.dt.from_np(v.dtype), kind="ExternalInput").ap())
    args.append(nc.dram_tensor("out_x", (NB * T, D), F32, kind="ExternalOutput").ap())
    block_kernel(nc, *args)
    r = run_bass_kernel_spmd(nc, [maps], core_ids=[0])
    return r.results[0]["out_x"].reshape(NB, T, D)
```
